# Optimizing a Trainium2 kernel written in Bass

```python
import numpy as np
import jax
import jax.numpy as jnp

def _softmax(x, axis=-1):
    return jax.nn.softmax(x, axis=axis)

def _gelu(x):
    return jax.nn.gelu(x, approximate=True)

def _silu(x):
    return jax.nn.silu(x)

def _sigmoid(x):
    return jax.nn.sigmoid(x)

def _layernorm(x, axis=-1, eps=1e-05):
    m = jnp.mean(x, axis=axis, keepdims=True)
    v = jnp.var(x, axis=axis, keepdims=True)
    return (x - m) / jnp.sqrt(v + eps)

def _scatter_add(tgt, idx, src, axis=0):
    return tgt.at[idx].add(src)

def _segment_sum(src, seg, n):
    return jax.ops.segment_sum(src, seg, n)
kernel_name = 'mk_gnn_preln_d1_gnn_r32_d2c505'

def setup_inputs(seed: int=0):
    np.random.seed(seed)
    _w = jnp.asarray

    def _rec_inputs():
        import jax
        import jax.numpy as jnp
        _gk = jax.random.key(seed)
        x = -0.0003713 + 1 * jax.random.normal(jax.random.fold_in(_gk, 1), (50000, 128), jnp.float32)
        src = jax.random.randint(jax.random.fold_in(_gk, 2), (25000,), 0, 50000, jnp.int32)
        dst = jnp.minimum((50000 * jax.random.uniform(jax.random.fold_in(_gk, 3), (25000,)) ** 2.0).astype(jnp.int32), 49999)
        _o = jnp.argsort(dst, stable=True)
        src = src[_o]
        dst = dst[_o]
        edge_attr_128 = 5.93493e-05 + 1.00006 * jax.random.normal(jax.random.fold_in(_gk, 11), (25000, 128), jnp.float32)
        return (x, src, dst, edge_attr_128)
    x, src, dst, edge_attr_128 = _rec_inputs()

    def _L0_gnn_setup():
        import jax, jax.numpy as jnp
        import numpy as np
        N_NODES = 3125
        N_EDGES = 18750
        D = 128
        H = 256
        LN_EPS = 1e-05
        key = jax.random.key(seed)
        ks = jax.random.split(key, 8)
        x = jax.random.normal(ks[0], (N_NODES, D), dtype=jnp.float32)
        edge_index = jax.random.randint(ks[1], (2, N_EDGES), 0, N_NODES, dtype=jnp.int64)
        edge_attr = jax.random.normal(ks[2], (N_EDGES, D), dtype=jnp.float32)
        s1 = 1.0 / np.sqrt(H)
        s2 = 1.0 / np.sqrt(H)
        W1 = jax.random.uniform(ks[3], (H, H), jnp.float32, -s1, s1)
        b1 = jax.random.uniform(ks[4], (H,), jnp.float32, -s1, s1)
        W2 = jax.random.uniform(ks[5], (H, D), jnp.float32, -s2, s2)
        b2 = jax.random.uniform(ks[6], (D,), jnp.float32, -s2, s2)
        ln_gamma = jnp.ones((D,), jnp.float32)
        ln_beta = jnp.zeros((D,), jnp.float32)
        return {'x': x, 'edge_index': edge_index, 'edge_attr': edge_attr, 'W1': W1, 'b1': b1, 'W2': W2, 'b2': b2, 'ln_gamma': ln_gamma, 'ln_beta': ln_beta}
    _L0_gnn_all = _L0_gnn_setup()
    _L0_gnn_in = {k: v for k, v in _L0_gnn_all.items() if k in ('W1', 'b1', 'W2', 'b2', 'ln_gamma', 'ln_beta')}
    del _L0_gnn_all
    return {'x': x, 'src': src, 'dst': dst, 'edge_attr_128': edge_attr_128, 'L0_gnn_W1': _L0_gnn_in['W1'], 'L0_gnn_b1': _L0_gnn_in['b1'], 'L0_gnn_W2': _L0_gnn_in['W2'], 'L0_gnn_b2': _L0_gnn_in['b2'], 'L0_gnn_ln_gamma': _L0_gnn_in['ln_gamma'], 'L0_gnn_ln_beta': _L0_gnn_in['ln_beta']}

def reference(x, src, dst, edge_attr_128, L0_gnn_W1, L0_gnn_b1, L0_gnn_W2, L0_gnn_b2, L0_gnn_ln_gamma, L0_gnn_ln_beta):
    import jax
    import jax.numpy as jnp

    def _L0_gnn_ref(x, edge_index, edge_attr, W1, b1, W2, b2, ln_gamma, ln_beta):
        import jax, jax.numpy as jnp
        import numpy as np
        N_NODES = 3125
        N_EDGES = 18750
        D = 128
        H = 256
        LN_EPS = 1e-05
        i = edge_index[0]
        agg = jax.ops.segment_sum(edge_attr, i, num_segments=x.shape[0])
        h = jnp.concatenate([x, agg], axis=-1)
        h = jax.nn.silu(h @ W1 + b1)
        h = h @ W2 + b2
        mu = jnp.mean(h, axis=-1, keepdims=True)
        var = jnp.mean(jnp.square(h - mu), axis=-1, keepdims=True)
        h = (h - mu) * jax.lax.rsqrt(var + LN_EPS) * ln_gamma + ln_beta
        return h + x
    edge_index = jnp.stack([src, dst])
    h = jnp.maximum(_layernorm(x, axis=-1), 0.0)
    x = x + _L0_gnn_ref(h, edge_index, edge_attr_128, L0_gnn_W1, L0_gnn_b1, L0_gnn_W2, L0_gnn_b2, L0_gnn_ln_gamma, L0_gnn_ln_beta)
    return x

_drawn_inputs = setup_inputs


def setup_inputs(seed=0):
    import zlib

    import numpy as np

    out = dict(_drawn_inputs(seed))
    spreads = {'L0_gnn_ln_gamma': (1.0, 0.2), 'L0_gnn_ln_beta': (0.0, 0.1)}
    factors = {}
    for name, (base, spread) in spreads.items():
        noise = np.random.default_rng([zlib.crc32(name.encode()), seed]).standard_normal(out[name].shape)
        drawn = base * np.exp(spread * noise) if base else spread * noise
        out[name] = jnp.asarray(drawn.astype(out[name].dtype))
    for name, factor in factors.items():
        out[name] = (out[name] * factor).astype(out[name].dtype)
    return out
```

```python
from contextlib import ExitStack

import concourse.bass as bass
from concourse import mybir

F32 = mybir.dt.float32
F32R = mybir.dt.float32r
F16 = mybir.dt.float16
BF16 = mybir.dt.bfloat16
I32 = mybir.dt.int32
U32 = mybir.dt.uint32
ALU = mybir.AluOpType
ACT = mybir.ActivationFunctionType
AX = mybir.AxisListType

P = 128
TILES = 8
HALF = TILES // 2
BLOCK = P * TILES
RING = 3
EPS = 1e-5
STREAMS = 2
CAP = P // STREAMS
BIG = 128.0
UNROLL = 14
LAG_ONE_HOT = 4
LAG_TABLE = 5
OUTSIDE = 1 << 20


class Turn:

    def __init__(self, engine, i):
        self.engine, self.i, self.known = engine, i, {}

    def times(self, factor):
        if factor not in self.known:
            self.known[factor] = self.engine.snap(self.i * factor)
        return self.known[factor]


class Block:

    def __init__(self, q, j, turn=None):
        self.q, self.j, self.turn = q, j, turn

    def plus(self, d):
        return Block(self.q + (self.j + d) // RING, (self.j + d) % RING, self.turn)

    def number(self, factor=1, more=0):
        fixed = factor * (self.q * RING + self.j) + more
        return self.turn.times(factor * RING) + fixed if self.turn else fixed

    def lap(self, factor, more=0):
        fixed = factor * self.q + more
        return self.turn.times(factor) + fixed if self.turn else fixed

    def half(self, c, factor=1, more=0):
        return self.number(2 * factor, factor * c + more)

    def is_number(self, n):
        return self.turn is None and self.number() == n


def at_least(engine, semaphore, value, apart=None):
    if isinstance(value, int):
        if value > 0:
            engine.wait_ge(semaphore, value)
    else:
        engine.wait_ge(semaphore, value)
        if apart is not None:
            engine.sem_inc(apart)


def gnn_layer(nc, x, src, edge_attr, W1, b1, W2, b2, gamma, beta, out):
    nodes, D = x.shape
    edges = edge_attr.shape[0]
    H = W1.shape[1]
    assert D == P and H == 2 * P and nodes % TILES == 0
    NB = -(-nodes // BLOCK)
    LAST_ROWS = (nodes - (NB - 1) * BLOCK) // TILES
    NT = NB * TILES
    EC = -(-edges // P)
    FULL = edges // EC
    REST = edges - FULL * EC
    TURNS = EC // UNROLL
    assert EC % UNROLL == 0 and UNROLL % 2 == 0 and NT <= 512
    LOOP_TURNS = (NB - RING - RING) // RING
    HEAD = RING
    TAIL = HEAD + LOOP_TURNS * RING

    with ExitStack() as ctx:
        def sb(name, shape, dt):
            return ctx.enter_context(nc.sbuf_tensor(name, shape, dt))

        def psum(name, shape, dt=F32):
            return ctx.enter_context(nc.psum_tensor(name, shape, dt))

        def sem(name):
            return ctx.enter_context(nc.semaphore(name))

        spill = nc.dram_tensor("spill", (NB * BLOCK, D), F32, kind="Internal").ap()

        ident = sb("ident", [P, P], F32)
        ident16 = sb("ident16", [P, P], F16)
        swap16 = sb("swap16", [P, P], F16)
        before = sb("before", [P, P], F16)
        others = sb("others", [P, P], F16)
        zeros16 = sb("zeros16", [P, P], F16)
        ones16 = sb("ones16", [P, P], BF16)
        iota_tile = sb("iota_tile", [P, NT], F16)
        iota_rank = sb("iota_rank", [P, CAP], F16)
        iota_node = sb("iota_node", [P, P], F32)
        own_node = sb("own_node", [P, NT], F32)
        own_slot = sb("own_slot", [P, 1], F32)
        neg_big = sb("neg_big", [P, 1], F32)
        half_neg = sb("half_neg", [P, TILES], F32)

        srci = sb("srci", [P, EC], I32)
        tmp_a = sb("tmp_a", [P, EC], I32)
        tmp_b = sb("tmp_b", [P, EC], I32)
        tmp_c = sb("tmp_c", [P, EC], I32)
        edge_no = sb("edge_no", [P, EC], I32)
        tile_of = sb("tile_of", [P, EC], F32)
        word1 = sb("word1", [P, EC], F32)
        word2 = sb("word2", [P, EC], F32)
        rank = sb("rank", [P, EC], F32)
        hot_tile = sb("hot_tile", [P, UNROLL, NT], F16)
        hot_slot = sb("hot_slot", [P, UNROLL, P], F16)
        junk_rank = sb("junk_rank", [P, STREAMS, NT], BF16)
        words = sb("words", [P, STREAMS, NT], F16)
        w2i = sb("w2i", [P, NT], I32)
        w2hi = sb("w2hi", [P, NT], I32)
        w2lo = sb("w2lo", [P, NT], I32)
        edge16 = sb("edge16", [P, NT], F32)
        edge_f = sb("edge_f", [P, NT], F32)
        empty = sb("empty", [P, NT], F32)
        own_part = sb("own_part", [P, NT], F32)
        slot_edge = sb("slot_edge", [P, NT], U32)
        slot_node = sb("slot_node", [P, NT], F32)
        most = sb("most", [P, 1], F32)
        over = sb("over", [P, 1], F32)
        spilled = sb("spilled", [P, 1], F32)
        kept = sb("kept", [P, 1], F32)
        spilled_i = sb("spilled_i", [P, 1], I32)

        w1f = sb("w1f", [P, 2, H], F32)
        w1h = sb("w1h", [P, 2, H], F32R)
        w1l = sb("w1l", [P, 2, H], F32R)
        w2f = sb("w2f", [P, 2, D], F32)
        w2c = sb("w2c", [P, 2, D], F32)
        w2mean = sb("w2mean", [P, 2], F32)
        b1c = sb("b1c", [P, 2], F32)
        b2f = sb("b2f", [P, D], F32)
        b2c = sb("b2c", [P, D], F32)
        b2mean = sb("b2mean", [P, 1], F32)
        b2p = [sb(f"b2p{i}", [P, D], BF16) for i in range(3)]
        b2r = [sb(f"b2r{i}", [P, D], F32) for i in range(2)]
        b2rows = sb("b2rows", [P, HALF, D], BF16)
        gammas = sb("gammas", [P, D], F32)
        betas = sb("betas", [P, D], F32)

        X = [sb(f"X{j}", [P, TILES, D], F32) for j in range(RING)]
        Z = [sb(f"Z{j}", [P, TILES, D], F32) for j in range(RING)]
        R = [sb(f"R{j}", [P, TILES, D], F32) for j in range(RING)]
        G = [sb(f"G{j}", [P, TILES, D], F32) for j in range(RING)]
        HOT = [sb(f"HOT{j}", [P, TILES, P], F32) for j in range(RING)]
        gather_rows = [sb(f"gather_rows{j}", [P, TILES], U32) for j in range(RING)]
        zh = [sb(f"zh{c}", [P, HALF * P], F32R) for c in range(2)]
        zl = [sb(f"zl{c}", [P, HALF * P], F32R) for c in range(2)]
        ah = [sb(f"ah{c}", [P, HALF * P], F32R) for c in range(2)]
        al = [sb(f"al{c}", [P, HALF * P], F32R) for c in range(2)]
        S = [sb(f"S{c}", [P, 2, HALF * P], F32) for c in range(2)]
        T = [sb(f"T{c}", [P, HALF, D], F32) for c in range(2)]
        stat = sb("stat", [P, TILES, 6], F32)
        msum = sb("msum", [P, TILES], F32)
        mdif = sb("mdif", [P, TILES], F32)
        m2 = sb("m2", [P, TILES], F32)
        mdd = sb("mdd", [P, TILES], F32)
        var1 = sb("var1", [P, TILES], F32)
        rstd1 = sb("rstd1", [P, TILES], F32)
        shift1 = sb("shift1", [P, TILES], F32)
        junk_sq = sb("junk_sq", [P, 2, HALF, D], F32)
        ssq = [sb(f"ssq{c}", [P, HALF], F32) for c in range(2)]
        var2 = [sb(f"var2{c}", [P, HALF], F32) for c in range(2)]
        rstd2 = [sb(f"rstd2{c}", [P, HALF], F32) for c in range(2)]

        bank = [psum(f"bank{i}", [P, 512]) for i in range(8)]
        zt, agg, pre, y = bank[0:2], bank[2:4], bank[4:6], bank[6:8]
        counts, table = bank[4:6], bank[6:8]
        slot_word = bank[0:2]

        src_loaded, weights_loaded, rows_loaded = sem("src_loaded"), sem("weights_loaded"), sem("rows_loaded")
        src_filled = sem("src_filled")
        pool_const, dve_const = sem("pool_const"), sem("dve_const")
        dve_step = sem("dve_step")
        w1h_ready = sem("w1h_ready")
        tile_hot, slot_hot = sem("tile_hot"), sem("slot_hot")
        counted, ranked, slot_free = sem("counted"), sem("ranked"), sem("slot_free")
        table_done, words_copied, words_placed = sem("table_done"), sem("words_copied"), sem("words_placed")
        over_known, spill_known, slots_ready = sem("over_known"), sem("spill_known"), sem("slots_ready")
        pool_step = sem("pool_step")
        spill_zeroed, spill_added = sem("spill_zeroed"), sem("spill_added")
        rows_named = sem("rows_named")
        x_loaded = [sem(f"x_loaded{j}") for j in range(RING)]
        stored = [sem(f"stored{j}") for j in range(RING)]
        gathered = [[sem(f"gathered{j}{c}") for c in range(2)] for j in range(RING)]
        var1_done, rstd1_done, z_done = sem("var1_done"), sem("rstd1_done"), sem("z_done")
        hot_done, zt_done, agg_done = sem("hot_done"), sem("zt_done"), sem("agg_done")
        zh_done, zl_done, ah_done, al_done = sem("zh_done"), sem("zl_done"), sem("ah_done"), sem("al_done")
        pre_done, silu_done, y_done = sem("pre_done"), sem("silu_done"), sem("y_done")
        ssq_done, rstd2_done, pool_var2 = sem("ssq_done"), sem("rstd2_done"), sem("pool_var2")
        xb_done, r_done, t_done, out_done = sem("xb_done"), sem("r_done"), sem("t_done"), sem("out_done")
        small = sem("small")
        sp_passed, pool_passed = sem("sp_passed"), sem("pool_passed")

        def run_blocks(engine, step):
            for n in range(HEAD):
                step(Block(n // RING, n % RING))
            with engine.Fori(0, LOOP_TURNS) as i:
                turn = Turn(engine, i)
                for j in range(RING):
                    step(Block(HEAD // RING, j, turn))
            for n in range(TAIL, NB):
                step(Block(n // RING, n % RING))

        def exists(b):
            return b.turn is not None or b.number() < NB

        def run_columns(engine, step, lag):
            for u in range(UNROLL):
                step(u, u)
            with engine.Fori(1, TURNS) as i:
                first = engine.snap(i * UNROLL)
                for u in range(UNROLL):
                    step(first + u, u)
            for u in range(lag):
                step(EC + u, u)

        def real(column):
            return not isinstance(column, int) or 0 <= column < EC

        block = ctx.enter_context(nc.Block())

        @block.sync
        def _(sp):
            sp.wait_ge(src_filled, 1)
            sp.dma_start(srci[0:FULL, :], src[0:FULL * EC].rearrange("(p c) -> p c", c=EC)).then_inc(src_loaded, 16)
            sp.dma_start(srci[FULL:FULL + 1, 0:REST],
                         src[FULL * EC:edges].rearrange("(p c) -> p c", p=1)).then_inc(src_loaded, 16)
            sp.dma_start(w1f[:], W1.rearrange("(k p) h -> p k h", p=P)).then_inc(weights_loaded, 16)
            sp.dma_start(w2f[:], W2.rearrange("(k p) d -> p k d", p=P)).then_inc(weights_loaded, 16)
            sp.dma_start(b1c[:], b1.rearrange("(k p) -> p k", p=P),
                         allow_slow_non_contiguous=True).then_inc(weights_loaded, 16)
            sp.dma_start(gammas[:], gamma.partition_broadcast(P)).then_inc(weights_loaded, 16)
            sp.dma_start(betas[:], beta.partition_broadcast(P)).then_inc(weights_loaded, 16)
            sp.dma_start(b2f[:], b2.partition_broadcast(P)).then_inc(weights_loaded, 16)

            def load(b):
                at_least(sp, z_done, b.number(1, 1 - RING), apart=sp_passed)
                at_least(sp, xb_done, b.half(0, 1, 2 - 2 * RING), apart=sp_passed)
                rows = LAST_ROWS if b.is_number(NB - 1) else P
                sp.dma_start(X[b.j][0:rows], x[bass.ds(b.number(BLOCK), rows * TILES), :]
                             .rearrange("(p t) d -> p t d", t=TILES)).then_inc(x_loaded[b.j], 16)

            def store(b):
                at_least(sp, out_done, b.half(0, 1, 2), apart=sp_passed)
                rows = LAST_ROWS if b.is_number(NB - 1) else P
                sp.dma_start(out[bass.ds(b.number(BLOCK), rows * TILES), :]
                             .rearrange("(p t) d -> p t d", t=TILES), R[b.j][0:rows]).then_inc(stored[b.j], 16)

            for n in range(RING):
                load(Block(0, n))

            def step(b):
                if exists(b.plus(RING)):
                    load(b.plus(RING))
                if not b.is_number(0):
                    store(b.plus(-1))

            run_blocks(sp, step)
            store(Block((NB - 1) // RING, (NB - 1) % RING))
            for j in range(RING):
                sp.wait_ge(stored[j], 16 * len(range(j, NB, RING)))

        @block.gpsimd
        def _(pool):
            nc.gpsimd.memset(srci[:], OUTSIDE).then_inc(src_filled, 1)
            nc.gpsimd.memset(ident[:], 0.0).then_inc(pool_step, 1)
            nc.gpsimd.memset(before[:], 1.0).then_inc(pool_step, 1)
            pool.wait_ge(pool_step, 2)
            nc.gpsimd.affine_select(out=ident[:], in_=ident[:], compare_op=ALU.not_equal, fill=1.0, base=0,
                                    pattern=[[-1, P]], channel_multiplier=1).then_inc(pool_step, 1)
            nc.gpsimd.affine_select(out=before[:], in_=before[:], compare_op=ALU.is_gt, fill=0.0, base=0,
                                    pattern=[[1, P]], channel_multiplier=-1).then_inc(pool_step, 1)
            pool.wait_ge(pool_step, 4)
            nc.gpsimd.affine_select(out=before[:], in_=before[:], compare_op=ALU.not_equal, fill=BIG, base=0,
                                    pattern=[[-1, P]], channel_multiplier=1).then_inc(pool_step, 1)
            small_iota = dict(base=0, allow_small_or_imprecise_dtypes=True)
            nc.gpsimd.iota(edge_no[:], [[1, EC]], base=0, channel_multiplier=EC)
            nc.gpsimd.iota(iota_tile[:], [[1, NT]], channel_multiplier=0, **small_iota)
            nc.gpsimd.iota(iota_rank[:], [[1, CAP]], channel_multiplier=0, **small_iota)
            nc.gpsimd.iota(iota_node[:], [[1, P]], channel_multiplier=0, **small_iota)
            nc.gpsimd.iota(own_slot[:], [[1, 1]], channel_multiplier=1, **small_iota)
            nc.gpsimd.iota(own_node[:], [[BLOCK, NB], [1, TILES]], channel_multiplier=TILES, **small_iota)
            nc.gpsimd.memset(half_neg[:], -0.5).then_inc(pool_const, 1)

            pool.wait_ge(over_known, 1)
            nc.gpsimd.partition_all_reduce(spilled[:], over[:], P, bass.bass_isa.ReduceOp.max).then_inc(spill_known, 1)
            pool.wait_ge(slots_ready, 1)
            flag = pool.value_load(spilled_i[0:1, 0:1], min_val=0, max_val=1)
            with pool.If(flag != 0):
                pool.wait_ge(rows_loaded, 1)
                rows_zeroed = P * TILES
                with pool.Fori(0, NB) as n:
                    pool.dma_start(spill[bass.ds(n * rows_zeroed, rows_zeroed), :]
                                   .rearrange("(p t) d -> p t d", t=TILES), G[0][:]).then_inc(spill_zeroed, 16)
                pool.wait_ge(spill_zeroed, 16 * NB)
                with pool.Fori(0, edges) as e:
                    node = pool.value_load(src[bass.ds(e, 1)].rearrange("(a b) -> a b", a=1),
                                           min_val=0, max_val=nodes - 1)
                    pool.dma_start(spill[bass.ds(node, 1), :], edge_attr[bass.ds(e, 1), :],
                                   accum_op=ALU.add).then_inc(spill_added, 16)
                    pool.wait_ge(spill_added, 16)
                    pool.sem_clear(spill_added)

            def gather(b, c):
                if c == 0:
                    nc.gpsimd.tensor_copy(gather_rows[b.j][:],
                                          slot_edge[:, bass.ds(b.number(TILES), TILES)]).then_inc(rows_named, 1)
                at_least(pool, agg_done, b.half(0, 1, 2 - 2 * RING), apart=pool_passed)
                at_least(pool, rows_named, b.number(1, 1), apart=pool_passed)

                def rows_from(source, last):
                    for t in range(c * HALF, (c + 1) * HALF):
                        nc.gpsimd.indirect_dma_start(
                            G[b.j][:, t, :], None, source,
                            bass.IndirectOffsetOnAxis(ap=gather_rows[b.j][:, t:t + 1], axis=0),
                            bounds_check=last, oob_is_err=False).then_inc(gathered[b.j][c], 16)

                with pool.If(flag != 0):
                    rows_from(spill, NB * BLOCK - 1)
                with pool.If(flag == 0):
                    rows_from(edge_attr, edges - 1)

            def power1(b):
                at_least(pool, var1_done, b.number(1, 1))
                nc.gpsimd.tensor_tensor(out=rstd1[:], in0=var1[:], in1=half_neg[:], op=ALU.pow).then_inc(rstd1_done, 1)

            def power2(b, c):
                at_least(pool, ssq_done, b.half(c, 1, 1), apart=pool_passed)
                at_least(pool, t_done, b.half(c, 1, -1), apart=pool_passed)
                nc.gpsimd.tensor_scalar(out=var2[c][:], in0=ssq[c][:], scalar1=1.0 / D, scalar2=EPS,
                                        op0=ALU.mult, op1=ALU.add).then_inc(pool_var2, 1)
                pool.wait_ge(pool_var2, b.half(c, 1, 1))
                nc.gpsimd.tensor_tensor(out=rstd2[c][:], in0=var2[c][:], in1=half_neg[:, 0:HALF],
                                        op=ALU.pow).then_inc(rstd2_done, 1)

            def x_plus_beta(b, c):
                pool.wait_ge(x_loaded[b.j], b.lap(16, 16))
                at_least(pool, stored[b.j], b.lap(16))
                s = slice(c * HALF, (c + 1) * HALF)
                nc.gpsimd.tensor_tensor(out=R[b.j][:, s, :], in0=X[b.j][:, s, :],
                                        in1=betas[:].unsqueeze(1).to_broadcast([P, HALF, D]),
                                        op=ALU.add).then_inc(xb_done, 1)

            pool.wait_ge(weights_loaded, 16 * 6)
            pool.wait_ge(rows_loaded, 1)
            for c in range(2):
                gather(Block(0, 0), c)
            power1(Block(0, 0))
            for c in range(2):
                x_plus_beta(Block(0, 0), c)
            power1(Block(0, 1))
            for c in range(2):
                gather(Block(0, 1), c)

            def step(b):
                for c in range(2):
                    if c or not b.is_number(0):
                        power2(b if c else b.plus(-1), 1 - c)
                    if exists(b.plus(2)):
                        gather(b.plus(2), c)
                        if c == 0:
                            power1(b.plus(2))
                    if exists(b.plus(1)):
                        x_plus_beta(b.plus(1), c)

            run_blocks(pool, step)
            power2(Block((NB - 1) // RING, (NB - 1) % RING), 1)

        @block.scalar
        def _(act):
            act.wait_ge(dve_const, 1)

            def rank_of(column, u):
                if not real(column):
                    return
                act.wait_ge(counted, column + 1)
                nc.scalar.activation(junk_rank[:, u % 2, :], counts[u % 2][:, 0:NT], ACT.Relu, bias=neg_big[:],
                                     accum_out=rank[:, bass.ds(column, 1)]).then_inc(ranked, 1)

            run_columns(act, rank_of, 0)
            act.wait_ge(weights_loaded, 16 * 6)
            nc.scalar.copy(w1h[:], w1f[:]).then_inc(w1h_ready, 1)

            def split_z(b, c):
                act.wait_ge(zt_done, b.half(c, 1, 1))
                at_least(act, pre_done, b.half(c, 2, -2))
                nc.scalar.activation(zh[c][:], zt[c][:], ACT.Relu).then_inc(zh_done, 1)

            def split_a(b, c):
                act.wait_ge(agg_done, b.half(c, 1, 1))
                nc.scalar.copy(ah[c][:], agg[c][:]).then_inc(ah_done, 1)

            def silu(b, c):
                for m in range(2):
                    act.wait_ge(pre_done, b.half(c, 2, m + 1))
                    at_least(act, y_done, b.half(c, 1, -1))
                    nc.scalar.activation(S[c][:, m, :], pre[m][:], ACT.Silu, bias=b1c[:, m:m + 1]).then_inc(silu_done, 1)

            def squares(b, c):
                act.wait_ge(y_done, b.half(c, 1, 1))
                at_least(act, rstd2_done, b.half(c, 1, -1))
                for t in range(HALF):
                    done = nc.scalar.activation(junk_sq[:, c, t, :], y[c][:, t * D:(t + 1) * D], ACT.Square,
                                                accum_out=ssq[c][:, t:t + 1])
                done.then_inc(ssq_done, 1)

            for c in range(2):
                split_z(Block(0, 0), c)
                split_a(Block(0, 0), c)

            def step(b):
                for c in range(2):
                    silu(b, c)
                    if exists(b.plus(1)):
                        split_z(b.plus(1), c)
                        split_a(b.plus(1), c)
                    squares(b, c)

            run_blocks(act, step)

        @block.tensor
        def _(pe):
            pe.wait_ge(dve_const, 2)
            for s in range(STREAMS):
                nc.tensor.matmul(counts[s][:, 0:NT], zeros16[:], iota_tile[:], start=True, stop=True)
                done = nc.tensor.matmul(table[s][:, 0:NT], zeros16[:], iota_tile[:], start=True, stop=True)
            done.then_inc(slot_free, UNROLL)

            def ring(u, lag):
                return (u - lag) % UNROLL

            def column_step(column, u):
                add = dict(start=False, stop=True, skip_group_check=True)
                if real(column - 2):
                    v = ring(u, 2)
                    pe.wait_ge(ranked, column - 1)
                    nc.tensor.matmul(counts[v % 2][:, 0:NT], others[:], hot_tile[:, v, :], **add)
                if real(column):
                    pe.wait_ge(tile_hot, column + 1)
                    nc.tensor.matmul(counts[u % 2][:, 0:NT], before[:], hot_tile[:, u, :], **add).then_inc(counted, 1)
                if real(column - LAG_TABLE):
                    v = ring(u, LAG_TABLE)
                    pe.wait_ge(slot_hot, column - LAG_TABLE + 1)
                    nc.tensor.matmul(table[v % 2][:, 0:NT], hot_slot[:, v, :], hot_tile[:, v, :],
                                     **add).then_inc(slot_free, 1)

            run_columns(pe, column_step, LAG_TABLE)

            pe.wait_ge(words_copied, 2)
            for w in range(2):
                rows = slice(w * CAP, (w + 1) * CAP)
                for s in range(STREAMS):
                    to = ident16 if w == s else swap16
                    done = nc.tensor.matmul(slot_word[w][:, 0:NT], to[rows, :], words[rows, s, :],
                                            start=(s == 0), stop=(s == STREAMS - 1))
                done.then_inc(words_placed, 1)

            def turn_z(b, c):
                pe.wait_ge(z_done, b.number(1, 1))
                at_least(pe, zh_done, b.half(c, 1, -1))
                at_least(pe, zl_done, b.half(c, 1, -1))
                for t in range(HALF):
                    done = nc.tensor.transpose(zt[c][:, t * P:(t + 1) * P], Z[b.j][:, c * HALF + t, :], ident[:])
                done.then_inc(zt_done, 1)

            def sum_edges(b, c):
                pe.wait_ge(gathered[b.j][c], b.lap(16 * HALF, 16 * HALF))
                pe.wait_ge(hot_done, b.half(c, 1, 1))
                at_least(pe, ah_done, b.half(c, 1, -1))
                at_least(pe, al_done, b.half(c, 1, -1))
                for t in range(HALF):
                    done = nc.tensor.matmul(agg[c][:, t * P:(t + 1) * P], G[b.j][:, c * HALF + t, :],
                                            HOT[b.j][:, c * HALF + t, :], start=True, stop=True)
                done.then_inc(agg_done, 1)

            def layer1(b, c):
                pe.wait_ge(zh_done, b.half(c, 1, 1))
                pe.wait_ge(zl_done, b.half(c, 1, 1))
                for m in range(2):
                    at_least(pe, silu_done, b.half(c, 2, m - 1))
                    cols = slice(m * P, (m + 1) * P)
                    nc.tensor.matmul(pre[m][:], w1h[:, 0, cols], zh[c][:], start=True, stop=False)
                    nc.tensor.matmul(pre[m][:], w1l[:, 0, cols], zh[c][:], start=False, stop=False)
                    nc.tensor.matmul(pre[m][:], w1h[:, 0, cols], zl[c][:], start=False, stop=False)
                    if m == 0:
                        pe.wait_ge(ah_done, b.half(c, 1, 1))
                        pe.wait_ge(al_done, b.half(c, 1, 1))
                    nc.tensor.matmul(pre[m][:], w1h[:, 1, cols], ah[c][:], start=False, stop=False)
                    nc.tensor.matmul(pre[m][:], w1l[:, 1, cols], ah[c][:], start=False, stop=False)
                    nc.tensor.matmul(pre[m][:], w1h[:, 1, cols], al[c][:], start=False, stop=True).then_inc(pre_done, 1)

            def layer2(b, c):
                at_least(pe, t_done, b.half(c, 1, -1))
                nc.tensor.matmul(y[c][:], ones16[:], b2rows[:].rearrange("p t d -> p (t d)"), start=True, stop=False)
                pe.wait_ge(silu_done, b.half(c, 2, 2))
                for t in range(HALF):
                    for m in range(2):
                        done = nc.tensor.matmul(y[c][:, t * D:(t + 1) * D], S[c][:, m, t * P:(t + 1) * P],
                                                w2c[:, m, :], start=False, stop=(t == HALF - 1 and m == 1))
                done.then_inc(y_done, 1)

            pe.wait_ge(slots_ready, 1)
            pe.wait_ge(dve_const, 3)
            pe.wait_ge(w1h_ready, 1)
            for c in range(2):
                turn_z(Block(0, 0), c)
                sum_edges(Block(0, 0), c)

            def step(b):
                for c in range(2):
                    layer1(b, c)
                    if exists(b.plus(1)):
                        turn_z(b.plus(1), c)
                        sum_edges(b.plus(1), c)
                    layer2(b, c)

            run_blocks(pe, step)

        @block.vector
        def _(dve):
            steps = [0]

            def link(instruction):
                steps[0] += 1
                instruction.then_inc(dve_step, 1)
                dve.wait_ge(dve_step, steps[0])

            nc.vector.memset(neg_big[:], -BIG).then_inc(dve_const, 1)
            nc.vector.memset(zeros16[:], 0.0)
            nc.vector.memset(ones16[:], 1.0)
            dve.wait_ge(pool_const, 1)
            nc.vector.tensor_copy(ident16[:], ident[:])
            nc.vector.tensor_copy(swap16[:, 0:CAP], ident[:, CAP:P])
            nc.vector.tensor_copy(swap16[:, CAP:P], ident[:, 0:CAP])
            nc.vector.tensor_scalar(out=others[:], in0=before[:], scalar1=-1.0, scalar2=1.0,
                                    op0=ALU.mult, op1=ALU.add).then_inc(dve_const, 1)

            dve.wait_ge(src_loaded, 32)

            def bits(dst, a, s1, o1, s2, o2):
                return nc.vector.tensor_scalar(out=dst[:], in0=a[:], scalar1=s1, scalar2=s2, op0=o1, op1=o2)

            shr, shl, band = ALU.logical_shift_right, ALU.logical_shift_left, ALU.bitwise_and
            bits(tmp_a, srci, 10, shr, 3, shl)
            link(bits(tmp_b, srci, TILES - 1, band, None, ALU.bypass))
            link(nc.vector.tensor_tensor(out=tile_of[:], in0=tmp_a[:], in1=tmp_b[:], op=ALU.add))
            bits(tmp_a, srci, 3, shr, P - 1, band)
            link(bits(tmp_b, edge_no, 15, band, 7, shl))
            nc.vector.tensor_tensor(out=word2[:], in0=tmp_a[:], in1=tmp_b[:], op=ALU.add)
            link(bits(tmp_c, edge_no, 4, shr, None, ALU.bypass))
            link(nc.vector.tensor_scalar(out=word1[:], in0=tmp_c[:], scalar1=1.0, scalar2=None, op0=ALU.add))

            def column_step(column, u):
                if real(column):
                    dve.wait_ge(slot_free, column + 1)
                    nc.vector.tensor_scalar(out=hot_tile[:, u, :], in0=iota_tile[:],
                                            scalar1=tile_of[:, bass.ds(column, 1)], scalar2=None,
                                            op0=ALU.is_equal).then_inc(tile_hot, 1)
                late = column - LAG_ONE_HOT
                if real(late):
                    v = (u - LAG_ONE_HOT) % UNROLL
                    dve.wait_ge(ranked, late + 1)
                    for w, word in enumerate((word1, word2)):
                        done = nc.vector.tensor_scalar(out=hot_slot[:, v, w * CAP:(w + 1) * CAP], in0=iota_rank[:],
                                                       scalar1=rank[:, bass.ds(late, 1)],
                                                       scalar2=word[:, bass.ds(late, 1)],
                                                       op0=ALU.is_equal, op1=ALU.mult)
                    done.then_inc(slot_hot, 1)

            run_columns(dve, column_step, LAG_ONE_HOT)

            link(nc.vector.tensor_reduce(out=most[:], in_=rank[:], axis=AX.X, op=ALU.max))
            nc.vector.tensor_scalar(out=over[:], in0=most[:], scalar1=CAP - 0.5, scalar2=None,
                                    op0=ALU.is_ge).then_inc(over_known, 1)
            dve.wait_ge(slot_free, EC + UNROLL)
            for s in range(STREAMS):
                nc.vector.tensor_copy(words[:, s, :], table[s][:, 0:NT]).then_inc(words_copied, 1)

            dve.wait_ge(w1h_ready, 1)
            dve.wait_ge(weights_loaded, 16 * 6)
            nc.vector.tensor_tensor(out=w1l[:], in0=w1f[:], in1=w1h[:].bitcast(F32), op=ALU.subtract)
            nc.vector.tensor_reduce(out=b2mean[:], in_=b2f[:], axis=AX.X, op=ALU.add)
            link(nc.vector.tensor_reduce(out=w2mean[:], in_=w2f[:], axis=AX.X, op=ALU.add))
            nc.vector.tensor_scalar(out=b2r[0][:], in0=b2f[:], scalar1=float(D), scalar2=b2mean[:],
                                    op0=ALU.mult, op1=ALU.subtract)
            for m in range(2):
                nc.vector.tensor_scalar(out=w2c[:, m, :], in0=w2f[:, m, :], scalar1=float(D),
                                        scalar2=w2mean[:, m:m + 1], op0=ALU.mult, op1=ALU.subtract)
            link(nc.vector.memset(b2rows[:], 0.0))
            link(nc.vector.tensor_scalar(out=w2c[:], in0=w2c[:], scalar1=1.0 / D, scalar2=None, op0=ALU.mult))
            link(nc.vector.tensor_scalar(out=b2c[:], in0=b2r[0][:], scalar1=1.0 / D, scalar2=None, op0=ALU.mult))
            link(nc.vector.tensor_copy(b2p[0][:], b2c[:]))
            link(nc.vector.tensor_tensor(out=b2r[0][:], in0=b2c[:], in1=b2p[0][:], op=ALU.subtract))
            link(nc.vector.tensor_copy(b2p[1][:], b2r[0][:]))
            link(nc.vector.tensor_tensor(out=b2r[1][:], in0=b2r[0][:], in1=b2p[1][:], op=ALU.subtract))
            link(nc.vector.tensor_copy(b2p[2][:], b2r[1][:]))
            for i in range(3):
                row = slice(32 * i, 32 * i + 1)
                for t in range(HALF):
                    done = nc.vector.tensor_copy(b2rows[row, t, :], b2p[i][row, :])
            done.then_inc(dve_const, 1)

            dve.wait_ge(words_placed, 2)
            nc.vector.tensor_copy(w2i[:], slot_word[1][:, 0:NT])
            nc.vector.tensor_scalar(out=empty[:], in0=slot_word[0][:, 0:NT], scalar1=0.0, scalar2=float(1 << 17),
                                    op0=ALU.is_equal, op1=ALU.mult)
            link(nc.vector.tensor_scalar(out=edge16[:], in0=slot_word[0][:, 0:NT], scalar1=-1.0, scalar2=16.0,
                                         op0=ALU.add, op1=ALU.mult))
            bits(w2hi, w2i, 7, shr, None, ALU.bypass)
            link(bits(w2lo, w2i, P - 1, band, None, ALU.bypass))
            nc.vector.tensor_tensor(out=edge_f[:], in0=edge16[:], in1=w2hi[:], op=ALU.add)
            link(nc.vector.tensor_tensor(out=slot_node[:], in0=empty[:], in1=w2lo[:], op=ALU.add))
            link(nc.vector.tensor_tensor(out=edge_f[:], in0=edge_f[:], in1=empty[:], op=ALU.add))
            dve.wait_ge(spill_known, 1)
            nc.vector.tensor_copy(spilled_i[:], spilled[:])
            link(nc.vector.tensor_scalar(out=kept[:], in0=spilled[:], scalar1=-1.0, scalar2=1.0,
                                         op0=ALU.mult, op1=ALU.add))
            nc.vector.tensor_scalar(out=own_part[:], in0=own_node[:], scalar1=spilled[:], scalar2=None, op0=ALU.mult)
            nc.vector.tensor_tensor(out=own_slot[:], in0=own_slot[:], in1=spilled[:], op=ALU.mult)
            link(nc.vector.tensor_scalar(out=edge_f[:], in0=edge_f[:], scalar1=kept[:], scalar2=None, op0=ALU.mult))
            nc.vector.tensor_scalar(out=slot_node[:], in0=slot_node[:], scalar1=kept[:], scalar2=own_slot[:],
                                    op0=ALU.mult, op1=ALU.add)
            link(nc.vector.tensor_tensor(out=slot_edge[:], in0=edge_f[:], in1=own_part[:], op=ALU.add))
            for j in range(RING):
                done = nc.vector.memset(G[j][:], 0.0)
            done.then_inc(rows_loaded, 1)
            nc.vector.engine_nop().then_inc(slots_ready, 1)

            SMALLS = 4

            def statistics(b):
                dve.wait_ge(x_loaded[b.j], b.lap(16, 16))
                for t in range(TILES):
                    done = nc.vector.bn_stats(stat[:, t, :], X[b.j][:, t, :])
                done.then_inc(small, 1)
                dve.wait_ge(small, b.number(SMALLS, 1))
                nc.vector.tensor_tensor(out=msum[:], in0=stat[:, :, 1], in1=stat[:, :, 4], op=ALU.add)
                nc.vector.tensor_tensor(out=mdif[:], in0=stat[:, :, 1], in1=stat[:, :, 4],
                                        op=ALU.subtract).then_inc(small, 1)
                nc.vector.scalar_tensor_tensor(out=m2[:], in0=stat[:, :, 2], scalar=EPS * D, in1=stat[:, :, 5],
                                               op0=ALU.add, op1=ALU.add)
                dve.wait_ge(small, b.number(SMALLS, 2))
                nc.vector.scalar_tensor_tensor(out=mdd[:], in0=mdif[:], scalar=0.25, in1=mdif[:],
                                               op0=ALU.mult, op1=ALU.mult).then_inc(small, 1)
                dve.wait_ge(small, b.number(SMALLS, 3))
                nc.vector.scalar_tensor_tensor(out=var1[:], in0=m2[:], scalar=1.0 / D, in1=mdd[:],
                                               op0=ALU.mult, op1=ALU.add).then_inc(var1_done, 1)

            def normalise(b):
                dve.wait_ge(rstd1_done, b.number(1, 1))
                nc.vector.scalar_tensor_tensor(out=shift1[:], in0=msum[:], scalar=-0.5, in1=rstd1[:],
                                               op0=ALU.mult, op1=ALU.mult).then_inc(small, 1)
                dve.wait_ge(small, b.number(SMALLS, 4))
                at_least(dve, zt_done, b.half(0, 1, 2 - 2 * RING))
                for t in range(TILES):
                    done = nc.vector.tensor_scalar(out=Z[b.j][:, t, :], in0=X[b.j][:, t, :], scalar1=rstd1[:, t:t + 1],
                                                   scalar2=shift1[:, t:t + 1], op0=ALU.mult, op1=ALU.add)
                done.then_inc(z_done, 1)

            def one_hots(b, c):
                at_least(dve, agg_done, b.half(0, 1, 2 - 2 * RING))
                nc.vector.tensor_tensor(
                    out=HOT[b.j][:, c * HALF:(c + 1) * HALF, :],
                    in0=iota_node[:].unsqueeze(1).to_broadcast([P, HALF, P]),
                    in1=slot_node[:, bass.ds(b.number(TILES, c * HALF), HALF)].unsqueeze(2).to_broadcast([P, HALF, P]),
                    op=ALU.is_equal).then_inc(hot_done, 1)

            def split_z(b, c):
                dve.wait_ge(zh_done, b.half(c, 1, 1))
                at_least(dve, pre_done, b.half(c, 2, -2))
                nc.vector.scalar_tensor_tensor(out=zl[c][:], in0=zt[c][:], scalar=0.0, in1=zh[c][:].bitcast(F32),
                                               op0=ALU.max, op1=ALU.subtract).then_inc(zl_done, 1)

            def split_a(b, c):
                dve.wait_ge(ah_done, b.half(c, 1, 1))
                nc.vector.tensor_tensor(out=al[c][:], in0=agg[c][:], in1=ah[c][:].bitcast(F32),
                                        op=ALU.subtract).then_inc(al_done, 1)

            def residual(b, c):
                dve.wait_ge(xb_done, b.half(c, 1, 1))
                dve.wait_ge(z_done, b.number(1, 1))
                s = slice(c * HALF, (c + 1) * HALF)
                nc.vector.scalar_tensor_tensor(out=R[b.j][:, s, :], in0=Z[b.j][:, s, :], scalar=0.0,
                                               in1=R[b.j][:, s, :], op0=ALU.max, op1=ALU.add).then_inc(r_done, 1)

            def result(b, c):
                dve.wait_ge(rstd2_done, b.half(c, 1, 1))
                at_least(dve, out_done, b.half(c, 1, -1))
                for t in range(HALF):
                    done = nc.vector.scalar_tensor_tensor(out=T[c][:, t, :], in0=y[c][:, t * D:(t + 1) * D],
                                                          scalar=rstd2[c][:, t:t + 1], in1=gammas[:],
                                                          op0=ALU.mult, op1=ALU.mult)
                done.then_inc(t_done, 1)
                dve.wait_ge(t_done, b.half(c, 1, 1))
                dve.wait_ge(r_done, b.half(c, 1, 1))
                s = slice(c * HALF, (c + 1) * HALF)
                nc.vector.tensor_tensor(out=R[b.j][:, s, :], in0=T[c][:], in1=R[b.j][:, s, :],
                                        op=ALU.add).then_inc(out_done, 1)

            for n in range(2):
                statistics(Block(0, n))
                normalise(Block(0, n))
                for c in range(2):
                    one_hots(Block(0, n), c)
                if n == 0:
                    split_z(Block(0, 0), 0)
                    split_a(Block(0, 0), 0)
            for c in range(2):
                residual(Block(0, 0), c)

            def step(b):
                for c in range(2):
                    ahead = b.plus(1) if c else b
                    if exists(ahead):
                        split_z(ahead, 1 - c)
                        split_a(ahead, 1 - c)
                    if exists(b.plus(2)):
                        one_hots(b.plus(2), c)
                        if c == 0:
                            statistics(b.plus(2))
                        else:
                            normalise(b.plus(2))
                    if c or not b.is_number(0):
                        result(b if c else b.plus(-1), 1 - c)
                    if exists(b.plus(1)):
                        residual(b.plus(1), c)

            run_blocks(dve, step)
            result(Block((NB - 1) // RING, (NB - 1) % RING), 1)


_INS = ['x', 'src', 'edge_attr_128', 'L0_gnn_W1', 'L0_gnn_b1', 'L0_gnn_W2', 'L0_gnn_b2', 'L0_gnn_ln_gamma',
        'L0_gnn_ln_beta']


def kernel(**inputs):
    import numpy as _np
    import concourse.bacc as _bacc
    from concourse import mybir as _mybir
    from concourse.bass_utils import run_bass_kernel_spmd as _run

    nc = _bacc.Bacc("TRN2", target_bir_lowering=False, num_devices=1)
    arrays, args = {}, []
    for name in _INS:
        a = _np.ascontiguousarray(inputs[name])
        arrays[f"in_{name}_dram"] = a
        args.append(nc.dram_tensor(f"in_{name}_dram", a.shape, _mybir.dt.from_np(a.dtype), kind="ExternalInput").ap())
    shape = _np.asarray(inputs['x']).shape
    args.append(nc.dram_tensor("out_dram", shape, _mybir.dt.float32, kind="ExternalOutput").ap())
    gnn_layer(nc, *args)
    r = _run(nc, [arrays], core_ids=[0])
    return r.results[0]["out_dram"]
```

```python
from contextlib import ExitStack

import concourse.bass as bass
from concourse import mybir

F32 = mybir.dt.float32
F32R = mybir.dt.float32r
F16 = mybir.dt.float16
BF16 = mybir.dt.bfloat16
I32 = mybir.dt.int32
U32 = mybir.dt.uint32
ALU = mybir.AluOpType
ACT = mybir.ActivationFunctionType
AX = mybir.AxisListType

P = 128
TILES = 8
HALF = TILES // 2
BLOCK = P * TILES
RING = 3
EPS = 1e-5
STREAMS = 2
CAP = P // STREAMS
BIG = 128.0
BATCH = 7
UNROLL = 4 * BATCH
LAG_TABLE = 2 * BATCH
TURN_BLOCKS = 6
RSQRT_SEED = 0x5F3759DF
NEWTON = 3
OUTSIDE = 1 << 20


class Turn:

    def __init__(self, engine, i):
        self.engine, self.i, self.known = engine, i, {}

    def times(self, factor):
        if factor not in self.known:
            self.known[factor] = self.engine.snap(self.i * factor)
        return self.known[factor]


class Item:

    def __init__(self, n, stride=0, turn=None):
        self.n, self.stride, self.turn = n, stride, turn

    def plus(self, d):
        return Item(self.n + d, self.stride, self.turn)

    def ring(self, size):
        assert self.stride % size == 0
        return self.n % size

    def number(self, factor=1, more=0):
        fixed = factor * self.n + more
        return self.turn.times(factor * self.stride) + fixed if self.turn else fixed

    def group(self, size, factor=1, more=0):
        assert self.stride % size == 0
        fixed = factor * (self.n // size) + more
        return self.turn.times(factor * self.stride // size) + fixed if self.turn else fixed

    def exists(self, count):
        return self.turn is not None or 0 <= self.n < count

    def is_number(self, n):
        return self.turn is None and self.n == n


class Block(Item):

    @property
    def j(self):
        return self.ring(RING)

    def plus(self, d):
        return Block(self.n + d, self.stride, self.turn)

    def lap(self, factor, more=0):
        return self.group(RING, factor, more)

    def half(self, c, factor=1, more=0):
        return self.number(2 * factor, factor * c + more)


def at_least(engine, semaphore, value, apart=None):
    if isinstance(value, int):
        if value > 0:
            engine.wait_ge(semaphore, value)
    else:
        engine.wait_ge(semaphore, value)
        if apart is not None:
            engine.sem_inc(apart)


def gnn_layer(nc, x, src, edge_attr, W1, b1, W2, b2, gamma, beta, out):
    nodes, D = x.shape
    edges = edge_attr.shape[0]
    H = W1.shape[1]
    assert D == P and H == 2 * P and nodes % TILES == 0
    NB = -(-nodes // BLOCK)
    LAST_ROWS = (nodes - (NB - 1) * BLOCK) // TILES
    NT = NB * TILES
    EC = -(-edges // P)
    FULL = edges // EC
    REST = edges - FULL * EC
    TURNS = EC // UNROLL
    assert EC % UNROLL == 0 and UNROLL % 2 == 0 and NT <= 512
    HEAD = RING
    LOOP_TURNS = (NB - HEAD - RING) // TURN_BLOCKS
    TAIL = HEAD + LOOP_TURNS * TURN_BLOCKS
    GROUP = max(n for n in range(1, 129) if edges % n == 0)

    with ExitStack() as ctx:
        def sb(name, shape, dt):
            return ctx.enter_context(nc.sbuf_tensor(name, shape, dt))

        def psum(name, shape, dt=F32):
            return ctx.enter_context(nc.psum_tensor(name, shape, dt))

        def sem(name):
            return ctx.enter_context(nc.semaphore(name))

        spill = nc.dram_tensor("spill", (NB * BLOCK, D), F32, kind="Internal").ap()

        ident = sb("ident", [P, P], F32)
        ident16 = sb("ident16", [P, P], F16)
        swap16 = sb("swap16", [P, P], F16)
        before = sb("before", [P, P], F16)
        others = sb("others", [P, P], F16)
        zeros16 = sb("zeros16", [P, P], F16)
        ones16 = sb("ones16", [P, P], BF16)
        iota_tile = sb("iota_tile", [P, NT], F16)
        iota_rank = sb("iota_rank", [P, CAP], F16)
        iota_node = sb("iota_node", [P, P], F32)
        own_node = sb("own_node", [P, NT], F32)
        own_slot = sb("own_slot", [P, 1], F32)
        neg_big = sb("neg_big", [P, 1], F32)

        srci = sb("srci", [P, EC], I32)
        tmp_a = sb("tmp_a", [P, EC], I32)
        tmp_b = sb("tmp_b", [P, EC], I32)
        tmp_c = sb("tmp_c", [P, EC], I32)
        edge_no = sb("edge_no", [P, EC], I32)
        tile_of = sb("tile_of", [P, EC], F32)
        word = sb("word", [P, EC, 2], F32)
        rank = sb("rank", [P, EC], F32)
        hot_tile = sb("hot_tile", [P, UNROLL, NT], F16)
        is_slot = sb("is_slot", [P, BATCH, CAP], F16)
        hot_slot = sb("hot_slot", [P, UNROLL, 2, CAP], F16)
        junk_rank = sb("junk_rank", [P, STREAMS, NT], BF16)
        words = sb("words", [P, STREAMS, NT], F16)
        w2i = sb("w2i", [P, NT], I32)
        w2hi = sb("w2hi", [P, NT], I32)
        w2lo = sb("w2lo", [P, NT], I32)
        edge16 = sb("edge16", [P, NT], F32)
        edge_f = sb("edge_f", [P, NT], F32)
        empty = sb("empty", [P, NT], F32)
        own_part = sb("own_part", [P, NT], F32)
        slot_edge = sb("slot_edge", [P, NT], U32)
        slot_node = sb("slot_node", [P, NT], F32)
        most = sb("most", [P, 1], F32)
        over = sb("over", [P, 1], F32)
        spilled = sb("spilled", [P, 1], F32)
        kept = sb("kept", [P, 1], F32)
        spilled_i = sb("spilled_i", [P, 1], I32)

        w1f = sb("w1f", [P, 2, H], F32)
        w1h = sb("w1h", [P, 2, H], F32R)
        w1l = sb("w1l", [P, 2, H], F32R)
        w2f = sb("w2f", [P, 2, D], F32)
        w2c = sb("w2c", [P, 2, D], F32)
        w2mean = sb("w2mean", [P, 2], F32)
        b1c = sb("b1c", [P, 2], F32)
        b2f = sb("b2f", [P, D], F32)
        b2c = sb("b2c", [P, D], F32)
        b2mean = sb("b2mean", [P, 1], F32)
        b2p = [sb(f"b2p{i}", [P, D], BF16) for i in range(3)]
        b2r = [sb(f"b2r{i}", [P, D], F32) for i in range(2)]
        b2rows = sb("b2rows", [P, HALF, D], BF16)
        gammas = sb("gammas", [P, D], F32)
        betas = sb("betas", [P, D], F32)

        X = [sb(f"X{j}", [P, TILES, D], F32) for j in range(RING)]
        H0 = [sb(f"H0{j}", [P, TILES, D], F32) for j in range(RING)]
        R = [sb(f"R{j}", [P, TILES, D], F32) for j in range(RING)]
        G = [sb(f"G{j}", [P, TILES, D], F32) for j in range(RING)]
        HOT = [sb(f"HOT{j}", [P, TILES, P], F32) for j in range(RING)]
        gather_rows = [sb(f"gather_rows{j}", [P, TILES], U32) for j in range(RING)]
        hi = [sb(f"hi{c}", [P, 2, HALF * P], F32R) for c in range(2)]
        lo = [sb(f"lo{c}", [P, 2, HALF * P], F32R) for c in range(2)]
        S = [sb(f"S{c}", [P, 2, HALF * P], F32) for c in range(2)]
        T = [sb(f"T{c}", [P, HALF, D], F32) for c in range(2)]
        stat = sb("stat", [P, TILES, 6], F32)
        msum = sb("msum", [P, TILES], F32)
        mdif = sb("mdif", [P, TILES], F32)
        m2 = sb("m2", [P, TILES], F32)
        mdd = sb("mdd", [P, TILES], F32)
        var = sb("var", [P, 2 * TILES], F32)
        bits_half = sb("bits_half", [P, 2 * TILES], I32)
        guess = [sb(f"guess{i}", [P, 2 * TILES], F32) for i in range(2)]
        guess_sq = sb("guess_sq", [P, 2 * TILES], F32)
        guess_off = sb("guess_off", [P, 2 * TILES], F32)
        rstd = [sb(f"rstd{j}", [P, 2 * TILES], F32) for j in range(RING)]
        shift = [sb(f"shift{j}", [P, TILES], F32) for j in range(RING)]
        meansq = [sb(f"meansq{j}", [P, TILES], F32) for j in range(RING)]
        junk_sq = sb("junk_sq", [P, 2, TILES, D], BF16)

        za = psum("za", [P, 2, HALF * P])
        pre = [psum(f"pre{m}", [P, 512]) for m in range(2)]
        y = [psum(f"y{i}", [P, 512]) for i in range(4)]
        counts, table = pre, y[0:2]
        slot_word = [za[:, w, :] for w in range(2)]

        src_loaded, weights_loaded = sem("src_loaded"), sem("weights_loaded")
        src_filled = sem("src_filled")
        pool_const, dve_const = sem("pool_const"), sem("dve_const")
        dve_step = sem("dve_step")
        w1h_ready = sem("w1h_ready")
        tile_hot, slot_step, slot_hot = sem("tile_hot"), sem("slot_step"), sem("slot_hot")
        counted, ranked, slot_free = sem("counted"), sem("ranked"), sem("slot_free")
        table_done, words_copied, words_placed = sem("table_done"), sem("words_copied"), sem("words_placed")
        over_known, spill_known, slots_ready = sem("over_known"), sem("spill_known"), sem("slots_ready")
        pool_step = sem("pool_step")
        spill_zeroed, spill_added = sem("spill_zeroed"), sem("spill_added")
        rows_named = sem("rows_named")
        x_loaded = [sem(f"x_loaded{j}") for j in range(RING)]
        stored = [sem(f"stored{j}") for j in range(RING)]
        gathered = [[sem(f"gathered{j}{c}") for c in range(2)] for j in range(RING)]
        bn_done, small, powers_done = sem("bn_done"), sem("small"), sem("powers_done")
        h0_done, turn_done, hot_done, agg_done = sem("h0_done"), sem("turn_done"), sem("hot_done"), sem("agg_done")
        hi_done, lo_done = sem("hi_done"), sem("lo_done")
        pre_done, silu_done, y_done = sem("pre_done"), sem("silu_done"), sem("y_done")
        squares_done = sem("squares_done")
        xb_done, r_done, t_done, out_done = sem("xb_done"), sem("r_done"), sem("t_done"), sem("out_done")
        sp_passed, pool_passed = sem("sp_passed"), sem("pool_passed")

        def run_blocks(engine, step):
            for n in range(HEAD):
                step(Block(n))
            with engine.Fori(0, LOOP_TURNS) as i:
                turn = Turn(engine, i)
                for n in range(HEAD, HEAD + TURN_BLOCKS):
                    step(Block(n, TURN_BLOCKS, turn))
            for n in range(TAIL, NB):
                step(Block(n))

        def run_columns(engine, step, lag):
            for n in range(UNROLL):
                step(Item(n))
            with engine.Fori(0, TURNS - 1) as i:
                turn = Turn(engine, i)
                for n in range(UNROLL, 2 * UNROLL):
                    step(Item(n, UNROLL, turn))
            for n in range(EC, EC + lag):
                step(Item(n))

        block = ctx.enter_context(nc.Block())

        @block.sync
        def _(sp):
            sp.wait_ge(src_filled, 1)
            sp.dma_start(srci[0:FULL, :], src[0:FULL * EC].rearrange("(p c) -> p c", c=EC)).then_inc(src_loaded, 16)
            sp.dma_start(srci[FULL:FULL + 1, 0:REST],
                         src[FULL * EC:edges].rearrange("(p c) -> p c", p=1)).then_inc(src_loaded, 16)
            sp.dma_start(w1f[:], W1.rearrange("(k p) h -> p k h", p=P)).then_inc(weights_loaded, 16)
            sp.dma_start(w2f[:], W2.rearrange("(k p) d -> p k d", p=P)).then_inc(weights_loaded, 16)
            sp.dma_start(b1c[:], b1.rearrange("(k p) -> p k", p=P),
                         allow_slow_non_contiguous=True).then_inc(weights_loaded, 16)
            sp.dma_start(gammas[:], gamma.partition_broadcast(P)).then_inc(weights_loaded, 16)
            sp.dma_start(betas[:], beta.partition_broadcast(P)).then_inc(weights_loaded, 16)
            sp.dma_start(b2f[:], b2.partition_broadcast(P)).then_inc(weights_loaded, 16)

            def load(b):
                at_least(sp, h0_done, b.half(0, 1, 2 - 2 * RING), apart=sp_passed)
                at_least(sp, xb_done, b.half(0, 1, 2 - 2 * RING), apart=sp_passed)
                rows = LAST_ROWS if b.is_number(NB - 1) else P
                sp.dma_start(X[b.j][0:rows], x[bass.ds(b.number(BLOCK), rows * TILES), :]
                             .rearrange("(p t) d -> p t d", t=TILES)).then_inc(x_loaded[b.j], 16)

            def store(b):
                at_least(sp, out_done, b.half(0, 1, 2), apart=sp_passed)
                rows = LAST_ROWS if b.is_number(NB - 1) else P
                sp.dma_start(out[bass.ds(b.number(BLOCK), rows * TILES), :]
                             .rearrange("(p t) d -> p t d", t=TILES), R[b.j][0:rows]).then_inc(stored[b.j], 16)

            for n in range(RING):
                load(Block(n))

            def step(b):
                if b.plus(RING).exists(NB):
                    load(b.plus(RING))
                if not b.is_number(0):
                    store(b.plus(-1))

            run_blocks(sp, step)
            store(Block(NB - 1))
            for j in range(RING):
                sp.wait_ge(stored[j], 16 * len(range(j, NB, RING)))

        @block.gpsimd
        def _(pool):
            nc.gpsimd.memset(srci[:], OUTSIDE).then_inc(src_filled, 1)
            nc.gpsimd.memset(ident[:], 0.0).then_inc(pool_step, 1)
            nc.gpsimd.memset(before[:], 1.0).then_inc(pool_step, 1)
            pool.wait_ge(pool_step, 2)
            nc.gpsimd.affine_select(out=ident[:], in_=ident[:], compare_op=ALU.not_equal, fill=1.0, base=0,
                                    pattern=[[-1, P]], channel_multiplier=1).then_inc(pool_step, 1)
            nc.gpsimd.affine_select(out=before[:], in_=before[:], compare_op=ALU.is_gt, fill=0.0, base=0,
                                    pattern=[[1, P]], channel_multiplier=-1).then_inc(pool_step, 1)
            pool.wait_ge(pool_step, 4)
            nc.gpsimd.affine_select(out=before[:], in_=before[:], compare_op=ALU.not_equal, fill=BIG, base=0,
                                    pattern=[[-1, P]], channel_multiplier=1).then_inc(pool_step, 1)
            small_iota = dict(base=0, allow_small_or_imprecise_dtypes=True)
            nc.gpsimd.iota(edge_no[:], [[1, EC]], base=0, channel_multiplier=EC)
            nc.gpsimd.iota(iota_tile[:], [[1, NT]], channel_multiplier=0, **small_iota)
            nc.gpsimd.iota(iota_rank[:], [[1, CAP]], channel_multiplier=0, **small_iota)
            nc.gpsimd.iota(iota_node[:], [[1, P]], channel_multiplier=0, **small_iota)
            nc.gpsimd.iota(own_slot[:], [[1, 1]], channel_multiplier=1, **small_iota)
            nc.gpsimd.iota(own_node[:], [[BLOCK, NB], [1, TILES]], channel_multiplier=TILES, **small_iota)
            for j in range(RING):
                done = nc.gpsimd.memset(G[j][:], 0.0)
            done.then_inc(pool_const, 1)

            pool.wait_ge(over_known, 1)
            nc.gpsimd.partition_all_reduce(spilled[:], over[:], P, bass.bass_isa.ReduceOp.max).then_inc(spill_known, 1)
            pool.wait_ge(slots_ready, 1)
            flag = pool.value_load(spilled_i[0:1, 0:1], min_val=0, max_val=1)
            with pool.If(flag != 0):
                pool.wait_ge(pool_const, 1)
                rows_zeroed = P * TILES
                with pool.Fori(0, NB) as n:
                    pool.dma_start(spill[bass.ds(n * rows_zeroed, rows_zeroed), :]
                                   .rearrange("(p t) d -> p t d", t=TILES), G[0][:]).then_inc(spill_zeroed, 16)
                pool.wait_ge(spill_zeroed, 16 * NB)
                with pool.Fori(0, edges // GROUP) as g:
                    first = pool.snap(g * GROUP)
                    with pool.Fori(0, GROUP) as i:
                        node = pool.value_load(src[bass.ds(first + i, 1)].rearrange("(a b) -> a b", a=1),
                                               min_val=0, max_val=nodes - 1)
                        pool.dma_start(spill[bass.ds(node, 1), :], edge_attr[bass.ds(first + i, 1), :],
                                       accum_op=ALU.add).then_inc(spill_added, 16)
                        at_least(pool, spill_added, i * 16 + 16, apart=pool_passed)
                    pool.dma_reset(range(spill_added.num, spill_added.num + 1))
                    pool.sem_clear(spill_added)

            def gather(b, c):
                at_least(pool, agg_done, b.half(0, 1, 2 - 2 * RING), apart=pool_passed)
                if c == 0:
                    nc.gpsimd.tensor_copy(gather_rows[b.j][:],
                                          slot_edge[:, bass.ds(b.number(TILES), TILES)]).then_inc(rows_named, 1)
                at_least(pool, rows_named, b.number(1, 1), apart=pool_passed)

                def rows_from(source, last):
                    for t in range(c * HALF, (c + 1) * HALF):
                        nc.gpsimd.indirect_dma_start(
                            G[b.j][:, t, :], None, source,
                            bass.IndirectOffsetOnAxis(ap=gather_rows[b.j][:, t:t + 1], axis=0),
                            bounds_check=last, oob_is_err=False).then_inc(gathered[b.j][c], 16)

                with pool.If(flag != 0):
                    rows_from(spill, NB * BLOCK - 1)
                with pool.If(flag == 0):
                    rows_from(edge_attr, edges - 1)

            def x_plus_beta(b, c):
                pool.wait_ge(x_loaded[b.j], b.lap(16, 16))
                at_least(pool, stored[b.j], b.lap(16))
                s = slice(c * HALF, (c + 1) * HALF)
                nc.gpsimd.tensor_tensor(out=R[b.j][:, s, :], in0=X[b.j][:, s, :],
                                        in1=betas[:].unsqueeze(1).to_broadcast([P, HALF, D]),
                                        op=ALU.add).then_inc(xb_done, 1)

            pool.wait_ge(weights_loaded, 16 * 6)
            pool.wait_ge(pool_const, 1)
            for c in range(2):
                gather(Block(0), c)
            for c in range(2):
                x_plus_beta(Block(0), c)
            for c in range(2):
                gather(Block(1), c)

            def step(b):
                for c in range(2):
                    if b.plus(2).exists(NB):
                        gather(b.plus(2), c)
                    if b.plus(1).exists(NB):
                        x_plus_beta(b.plus(1), c)

            run_blocks(pool, step)

        @block.scalar
        def _(act):
            act.wait_ge(dve_const, 1)

            def rank_of(column):
                s = column.ring(STREAMS)
                act.wait_ge(counted, column.number(1, 1))
                nc.scalar.activation(junk_rank[:, s, :], counts[s][:, 0:NT], ACT.Relu, bias=neg_big[:],
                                     accum_out=rank[:, bass.ds(column.number(), 1)]).then_inc(ranked, 1)

            run_columns(act, rank_of, 0)
            act.wait_ge(weights_loaded, 16 * 6)
            nc.scalar.copy(w1h[:], w1f[:]).then_inc(w1h_ready, 1)

            def normalise(b, c):
                act.wait_ge(powers_done, b.number(1, 1))
                at_least(act, turn_done, b.half(c, 1, 1 - 2 * RING))
                at_least(act, r_done, b.half(c, 1, 1 - 2 * RING))
                for t in range(c * HALF, (c + 1) * HALF):
                    done = nc.scalar.activation(H0[b.j][:, t, :], X[b.j][:, t, :], ACT.Relu,
                                                bias=shift[b.j][:, t:t + 1], scale=rstd[b.j][:, t:t + 1])
                done.then_inc(h0_done, 1)

            def split_high(b, c):
                act.wait_ge(turn_done, b.half(c, 1, 1))
                act.wait_ge(agg_done, b.half(c, 1, 1))
                at_least(act, pre_done, b.half(c, 2, -2))
                nc.scalar.copy(hi[c][:], za[:]).then_inc(hi_done, 1)

            def silu(b, c):
                for m in range(2):
                    act.wait_ge(pre_done, b.half(c, 2, m + 1))
                    at_least(act, y_done, b.half(c, 1, -1))
                    nc.scalar.activation(S[c][:, m, :], pre[m][:], ACT.Silu, bias=b1c[:, m:m + 1]).then_inc(silu_done, 1)

            def squares(b, c):
                p = b.ring(2)
                act.wait_ge(y_done, b.half(c, 1, 1))
                for t in range(HALF):
                    done = nc.scalar.activation(junk_sq[:, p, c * HALF + t, :], y[2 * p + c][:, t * D:(t + 1) * D], ACT.Square,
                                                scale=float(D) ** -0.5,
                                                accum_out=meansq[b.j][:, c * HALF + t:c * HALF + t + 1])
                done.then_inc(squares_done, 1)

            for c in range(2):
                normalise(Block(0), c)
            split_high(Block(0), 0)
            normalise(Block(1), 0)

            def step(b):
                for c in range(2):
                    silu(b, c)
                    ahead = b.plus(1) if c else b
                    if ahead.exists(NB):
                        split_high(ahead, 1 - c)
                    if b.plus(1 + c).exists(NB):
                        normalise(b.plus(1 + c), 1 - c)
                    squares(b, c)

            run_blocks(act, step)

        @block.tensor
        def _(pe):
            pe.wait_ge(dve_const, 2)
            for s in range(STREAMS):
                nc.tensor.matmul(counts[s][:, 0:NT], zeros16[:], iota_tile[:], start=True, stop=True)
                done = nc.tensor.matmul(table[s][:, 0:NT], zeros16[:], iota_tile[:], start=True, stop=True)
            done.then_inc(slot_free, UNROLL)

            add = dict(start=False, stop=True, skip_group_check=True)

            def column_step(column):
                early, late = column.plus(-2), column.plus(-LAG_TABLE)
                if early.exists(EC):
                    pe.wait_ge(ranked, early.number(1, 1))
                    nc.tensor.matmul(counts[early.ring(STREAMS)][:, 0:NT], others[:],
                                     hot_tile[:, early.ring(UNROLL), :], **add)
                if column.exists(EC):
                    pe.wait_ge(tile_hot, column.number(1, 1))
                    nc.tensor.matmul(counts[column.ring(STREAMS)][:, 0:NT], before[:],
                                     hot_tile[:, column.ring(UNROLL), :], **add).then_inc(counted, 1)
                if late.exists(EC):
                    pe.wait_ge(slot_hot, late.group(BATCH, 1, 1))
                    nc.tensor.matmul(table[late.ring(STREAMS)][:, 0:NT],
                                     hot_slot[:, late.ring(UNROLL)].rearrange("p w r -> p (w r)"),
                                     hot_tile[:, late.ring(UNROLL), :], **add).then_inc(slot_free, 1)

            run_columns(pe, column_step, LAG_TABLE)

            pe.wait_ge(words_copied, 2)
            for w in range(2):
                rows = slice(w * CAP, (w + 1) * CAP)
                for s in range(STREAMS):
                    to = ident16 if w == s else swap16
                    done = nc.tensor.matmul(slot_word[w][:, 0:NT], to[rows, :], words[rows, s, :],
                                            start=(s == 0), stop=(s == STREAMS - 1))
                done.then_inc(words_placed, 1)

            def turn_h(b, c):
                pe.wait_ge(h0_done, b.half(c, 1, 1))
                at_least(pe, hi_done, b.half(c))
                at_least(pe, lo_done, b.half(c))
                for t in range(HALF):
                    done = nc.tensor.transpose(za[:, 0, t * P:(t + 1) * P], H0[b.j][:, c * HALF + t, :], ident[:])
                done.then_inc(turn_done, 1)

            def sum_edges(b, c):
                pe.wait_ge(gathered[b.j][c], b.lap(16 * HALF, 16 * HALF))
                pe.wait_ge(hot_done, b.half(c, 1, 1))
                for t in range(HALF):
                    done = nc.tensor.matmul(za[:, 1, t * P:(t + 1) * P], G[b.j][:, c * HALF + t, :],
                                            HOT[b.j][:, c * HALF + t, :], start=True, stop=True)
                done.then_inc(agg_done, 1)

            def layer1(b, c):
                pe.wait_ge(hi_done, b.half(c, 1, 1))
                for m in range(2):
                    at_least(pe, silu_done, b.half(c, 2, m - 1))
                    cols = slice(m * P, (m + 1) * P)
                    for k in range(2):
                        nc.tensor.matmul(pre[m][:], w1h[:, k, cols], hi[c][:, k, :], start=(k == 0), stop=False)
                        nc.tensor.matmul(pre[m][:], w1l[:, k, cols], hi[c][:, k, :], start=False, stop=False)
                    if m == 0:
                        pe.wait_ge(lo_done, b.half(c, 1, 1))
                    for k in range(2):
                        done = nc.tensor.matmul(pre[m][:], w1h[:, k, cols], lo[c][:, k, :], start=False, stop=(k == 1))
                    done.then_inc(pre_done, 1)

            def layer2(b, c):
                place = y[2 * b.ring(2) + c]
                at_least(pe, t_done, b.half(c, 1, -3))
                nc.tensor.matmul(place[:], ones16[:], b2rows[:].rearrange("p t d -> p (t d)"), start=True, stop=False)
                pe.wait_ge(silu_done, b.half(c, 2, 2))
                for t in range(HALF):
                    for m in range(2):
                        done = nc.tensor.matmul(place[:, t * D:(t + 1) * D], S[c][:, m, t * P:(t + 1) * P],
                                                w2c[:, m, :], start=False, stop=(t == HALF - 1 and m == 1))
                done.then_inc(y_done, 1)

            pe.wait_ge(slots_ready, 1)
            pe.wait_ge(dve_const, 3)
            pe.wait_ge(w1h_ready, 1)
            turn_h(Block(0), 0)
            sum_edges(Block(0), 0)

            def step(b):
                for c in range(2):
                    layer1(b, c)
                    ahead = b.plus(1) if c else b
                    if ahead.exists(NB):
                        turn_h(ahead, 1 - c)
                        sum_edges(ahead, 1 - c)
                    layer2(b, c)

            run_blocks(pe, step)

        @block.vector
        def _(dve):
            steps = [0]

            def link(instruction):
                steps[0] += 1
                instruction.then_inc(dve_step, 1)
                dve.wait_ge(dve_step, steps[0])

            nc.vector.memset(neg_big[:], -BIG).then_inc(dve_const, 1)
            nc.vector.memset(zeros16[:], 0.0)
            nc.vector.memset(ones16[:], 1.0)
            for j in range(RING):
                nc.vector.memset(meansq[j][:], 1.0)
            dve.wait_ge(pool_const, 1)
            nc.vector.tensor_copy(ident16[:], ident[:])
            nc.vector.tensor_copy(swap16[:, 0:CAP], ident[:, CAP:P])
            nc.vector.tensor_copy(swap16[:, CAP:P], ident[:, 0:CAP])
            nc.vector.tensor_scalar(out=others[:], in0=before[:], scalar1=-1.0, scalar2=1.0,
                                    op0=ALU.mult, op1=ALU.add).then_inc(dve_const, 1)

            dve.wait_ge(src_loaded, 32)

            def bits(dst, a, s1, o1, s2, o2):
                return nc.vector.tensor_scalar(out=dst[:], in0=a[:], scalar1=s1, scalar2=s2, op0=o1, op1=o2)

            shr, shl, band = ALU.logical_shift_right, ALU.logical_shift_left, ALU.bitwise_and
            bits(tmp_a, srci, 10, shr, 3, shl)
            link(bits(tmp_b, srci, TILES - 1, band, None, ALU.bypass))
            link(nc.vector.tensor_tensor(out=tile_of[:], in0=tmp_a[:], in1=tmp_b[:], op=ALU.add))
            bits(tmp_a, srci, 3, shr, P - 1, band)
            link(bits(tmp_b, edge_no, 15, band, 7, shl))
            nc.vector.tensor_tensor(out=word[:, :, 1], in0=tmp_a[:], in1=tmp_b[:], op=ALU.add)
            link(bits(tmp_c, edge_no, 4, shr, None, ALU.bypass))
            link(nc.vector.tensor_scalar(out=word[:, :, 0], in0=tmp_c[:], scalar1=1.0, scalar2=None, op0=ALU.add))

            def column_step(column):
                if column.exists(EC):
                    dve.wait_ge(slot_free, column.number(1, 1))
                    nc.vector.tensor_scalar(out=hot_tile[:, column.ring(UNROLL), :], in0=iota_tile[:],
                                            scalar1=tile_of[:, bass.ds(column.number(), 1)], scalar2=None,
                                            op0=ALU.is_equal).then_inc(tile_hot, 1)
                late = column.plus(1 - 2 * BATCH)
                if column.ring(BATCH) == BATCH - 1 and late.exists(EC):
                    place = late.ring(UNROLL)
                    dve.wait_ge(ranked, late.number(1, BATCH))
                    at_least(dve, slot_hot, late.group(BATCH))
                    nc.vector.tensor_tensor(
                        out=is_slot[:], in0=iota_rank[:].unsqueeze(1).to_broadcast([P, BATCH, CAP]),
                        in1=rank[:, bass.ds(late.number(), BATCH)].unsqueeze(2).to_broadcast([P, BATCH, CAP]),
                        op=ALU.is_equal).then_inc(slot_step, 1)
                    dve.wait_ge(slot_step, late.group(BATCH, 1, 1))
                    nc.vector.tensor_tensor(
                        out=hot_slot[:, place:place + BATCH],
                        in0=is_slot[:].unsqueeze(2).to_broadcast([P, BATCH, 2, CAP]),
                        in1=word[:, bass.ds(late.number(), BATCH), :].unsqueeze(3).to_broadcast([P, BATCH, 2, CAP]),
                        op=ALU.mult).then_inc(slot_hot, 1)

            run_columns(dve, column_step, BATCH)

            link(nc.vector.tensor_reduce(out=most[:], in_=rank[:], axis=AX.X, op=ALU.max))
            nc.vector.tensor_scalar(out=over[:], in0=most[:], scalar1=CAP - 0.5, scalar2=None,
                                    op0=ALU.is_ge).then_inc(over_known, 1)

            def statistics(b):
                dve.wait_ge(x_loaded[b.j], b.lap(16, 16))
                at_least(dve, powers_done, b.number())
                for t in range(TILES):
                    done = nc.vector.bn_stats(stat[:, t, :], X[b.j][:, t, :])
                done.then_inc(bn_done, 1)

            SMALLS = 5 + 3 * NEWTON

            def powers(b):
                count = [0]

                def link_small(instruction):
                    count[0] += 1
                    instruction.then_inc(small, 1)
                    dve.wait_ge(small, b.number(SMALLS, count[0]))

                if b.exists(NB):
                    dve.wait_ge(bn_done, b.number(1, 1))
                    nc.vector.tensor_tensor(out=msum[:], in0=stat[:, :, 1], in1=stat[:, :, 4], op=ALU.add)
                    nc.vector.scalar_tensor_tensor(out=m2[:], in0=stat[:, :, 2], scalar=EPS * D, in1=stat[:, :, 5],
                                                   op0=ALU.add, op1=ALU.add)
                link_small(nc.vector.tensor_tensor(out=mdif[:], in0=stat[:, :, 1], in1=stat[:, :, 4],
                                                   op=ALU.subtract))
                link_small(nc.vector.scalar_tensor_tensor(out=mdd[:], in0=mdif[:], scalar=0.25, in1=mdif[:],
                                                          op0=ALU.mult, op1=ALU.mult))
                at_least(dve, squares_done, b.half(0, 1, 2 - 2 * RING))
                nc.vector.tensor_scalar(out=var[:, TILES:], in0=meansq[b.j][:], scalar1=EPS, scalar2=None, op0=ALU.add)
                link_small(nc.vector.scalar_tensor_tensor(out=var[:, 0:TILES], in0=m2[:], scalar=1.0 / D, in1=mdd[:],
                                                          op0=ALU.mult, op1=ALU.add))
                link_small(nc.vector.tensor_scalar(out=bits_half[:], in0=var[:].bitcast(I32), scalar1=1, scalar2=None,
                                                   op0=ALU.logical_shift_right, op1=ALU.bypass))
                link_small(nc.vector.tensor_scalar(out=guess[0][:].bitcast(I32), in0=bits_half[:], scalar1=-1.0,
                                                   scalar2=float(RSQRT_SEED), op0=ALU.mult, op1=ALU.add))
                for i in range(NEWTON):
                    now = guess[i % 2]
                    then = rstd[b.j] if i == NEWTON - 1 else guess[(i + 1) % 2]
                    link_small(nc.vector.scalar_tensor_tensor(out=guess_sq[:], in0=now[:], scalar=-0.5, in1=now[:],
                                                              op0=ALU.mult, op1=ALU.mult))
                    link_small(nc.vector.tensor_tensor(out=guess_off[:], in0=guess_sq[:], in1=var[:], op=ALU.mult))
                    link_small(nc.vector.scalar_tensor_tensor(out=then[:], in0=guess_off[:], scalar=1.5, in1=now[:],
                                                              op0=ALU.add, op1=ALU.mult))
                nc.vector.scalar_tensor_tensor(out=shift[b.j][:], in0=msum[:], scalar=-0.5, in1=rstd[b.j][:, 0:TILES],
                                               op0=ALU.mult, op1=ALU.mult).then_inc(powers_done, 1)

            statistics(Block(0))
            powers(Block(0))
            dve.wait_ge(slot_free, EC + UNROLL)
            for s in range(STREAMS):
                nc.vector.tensor_copy(words[:, s, :], table[s][:, 0:NT]).then_inc(words_copied, 1)
            statistics(Block(1))
            powers(Block(1))

            dve.wait_ge(w1h_ready, 1)
            dve.wait_ge(weights_loaded, 16 * 6)
            nc.vector.tensor_tensor(out=w1l[:], in0=w1f[:], in1=w1h[:].bitcast(F32), op=ALU.subtract)
            nc.vector.tensor_reduce(out=b2mean[:], in_=b2f[:], axis=AX.X, op=ALU.add)
            link(nc.vector.tensor_reduce(out=w2mean[:], in_=w2f[:], axis=AX.X, op=ALU.add))
            nc.vector.tensor_scalar(out=b2r[0][:], in0=b2f[:], scalar1=float(D), scalar2=b2mean[:],
                                    op0=ALU.mult, op1=ALU.subtract)
            for m in range(2):
                nc.vector.tensor_scalar(out=w2c[:, m, :], in0=w2f[:, m, :], scalar1=float(D),
                                        scalar2=w2mean[:, m:m + 1], op0=ALU.mult, op1=ALU.subtract)
            link(nc.vector.memset(b2rows[:], 0.0))
            link(nc.vector.tensor_scalar(out=w2c[:], in0=w2c[:], scalar1=1.0 / D, scalar2=None, op0=ALU.mult))
            link(nc.vector.tensor_scalar(out=b2c[:], in0=b2r[0][:], scalar1=1.0 / D, scalar2=None, op0=ALU.mult))
            link(nc.vector.tensor_copy(b2p[0][:], b2c[:]))
            link(nc.vector.tensor_tensor(out=b2r[0][:], in0=b2c[:], in1=b2p[0][:], op=ALU.subtract))
            link(nc.vector.tensor_copy(b2p[1][:], b2r[0][:]))
            link(nc.vector.tensor_tensor(out=b2r[1][:], in0=b2r[0][:], in1=b2p[1][:], op=ALU.subtract))
            link(nc.vector.tensor_copy(b2p[2][:], b2r[1][:]))
            for i in range(3):
                row = slice(32 * i, 32 * i + 1)
                for t in range(HALF):
                    done = nc.vector.tensor_copy(b2rows[row, t, :], b2p[i][row, :])
            done.then_inc(dve_const, 1)

            dve.wait_ge(words_placed, 2)
            nc.vector.tensor_copy(w2i[:], slot_word[1][:, 0:NT])
            nc.vector.tensor_scalar(out=empty[:], in0=slot_word[0][:, 0:NT], scalar1=0.0, scalar2=float(1 << 17),
                                    op0=ALU.is_equal, op1=ALU.mult)
            link(nc.vector.tensor_scalar(out=edge16[:], in0=slot_word[0][:, 0:NT], scalar1=-1.0, scalar2=16.0,
                                         op0=ALU.add, op1=ALU.mult))
            bits(w2hi, w2i, 7, shr, None, ALU.bypass)
            link(bits(w2lo, w2i, P - 1, band, None, ALU.bypass))
            nc.vector.tensor_tensor(out=edge_f[:], in0=edge16[:], in1=w2hi[:], op=ALU.add)
            link(nc.vector.tensor_tensor(out=slot_node[:], in0=empty[:], in1=w2lo[:], op=ALU.add))
            link(nc.vector.tensor_tensor(out=edge_f[:], in0=edge_f[:], in1=empty[:], op=ALU.add))
            dve.wait_ge(spill_known, 1)
            nc.vector.tensor_copy(spilled_i[:], spilled[:])
            link(nc.vector.tensor_scalar(out=kept[:], in0=spilled[:], scalar1=-1.0, scalar2=1.0,
                                         op0=ALU.mult, op1=ALU.add))
            nc.vector.tensor_scalar(out=own_part[:], in0=own_node[:], scalar1=spilled[:], scalar2=None, op0=ALU.mult)
            nc.vector.tensor_tensor(out=own_slot[:], in0=own_slot[:], in1=spilled[:], op=ALU.mult)
            link(nc.vector.tensor_scalar(out=edge_f[:], in0=edge_f[:], scalar1=kept[:], scalar2=None, op0=ALU.mult))
            nc.vector.tensor_scalar(out=slot_node[:], in0=slot_node[:], scalar1=kept[:], scalar2=own_slot[:],
                                    op0=ALU.mult, op1=ALU.add)
            link(nc.vector.tensor_tensor(out=slot_edge[:], in0=edge_f[:], in1=own_part[:], op=ALU.add))
            nc.vector.engine_nop().then_inc(slots_ready, 1)

            def one_hots(b, c):
                at_least(dve, agg_done, b.half(0, 1, 2 - 2 * RING))
                nc.vector.tensor_tensor(
                    out=HOT[b.j][:, c * HALF:(c + 1) * HALF, :],
                    in0=iota_node[:].unsqueeze(1).to_broadcast([P, HALF, P]),
                    in1=slot_node[:, bass.ds(b.number(TILES, c * HALF), HALF)].unsqueeze(2).to_broadcast([P, HALF, P]),
                    op=ALU.is_equal).then_inc(hot_done, 1)

            def split_low(b, c):
                dve.wait_ge(hi_done, b.half(c, 1, 1))
                at_least(dve, pre_done, b.half(c, 2, -2))
                nc.vector.tensor_tensor(out=lo[c][:], in0=za[:], in1=hi[c][:].bitcast(F32),
                                        op=ALU.subtract).then_inc(lo_done, 1)

            def residual(b, c):
                dve.wait_ge(xb_done, b.half(c, 1, 1))
                dve.wait_ge(h0_done, b.half(c, 1, 1))
                s = slice(c * HALF, (c + 1) * HALF)
                nc.vector.tensor_tensor(out=R[b.j][:, s, :], in0=H0[b.j][:, s, :], in1=R[b.j][:, s, :],
                                        op=ALU.add).then_inc(r_done, 1)

            def results(b):
                dve.wait_ge(powers_done, b.number(1, 1 + RING))
                at_least(dve, out_done, b.half(0))
                for c in range(2):
                    for t in range(HALF):
                        n = TILES + c * HALF + t
                        done = nc.vector.scalar_tensor_tensor(
                            out=T[c][:, t, :], in0=y[2 * b.ring(2) + c][:, t * D:(t + 1) * D],
                            scalar=rstd[b.j][:, n:n + 1], in1=gammas[:], op0=ALU.mult, op1=ALU.mult)
                    done.then_inc(t_done, 1)
                for c in range(2):
                    dve.wait_ge(t_done, b.half(c, 1, 1))
                    dve.wait_ge(r_done, b.half(c, 1, 1))
                    s = slice(c * HALF, (c + 1) * HALF)
                    nc.vector.tensor_tensor(out=R[b.j][:, s, :], in0=T[c][:], in1=R[b.j][:, s, :],
                                            op=ALU.add).then_inc(out_done, 1)

            for c in range(2):
                one_hots(Block(0), c)
            split_low(Block(0), 0)
            for c in range(2):
                one_hots(Block(1), c)
            for c in range(2):
                residual(Block(0), c)

            def step(b):
                split_low(b, 1)
                if b.plus(2).exists(NB):
                    statistics(b.plus(2))
                powers(b.plus(2))
                if b.plus(2).exists(NB):
                    one_hots(b.plus(2), 0)
                if b.plus(1).exists(NB):
                    residual(b.plus(1), 0)
                    split_low(b.plus(1), 0)
                if not b.is_number(0):
                    results(b.plus(-1))
                if b.plus(2).exists(NB):
                    one_hots(b.plus(2), 1)
                if b.plus(1).exists(NB):
                    residual(b.plus(1), 1)

            run_blocks(dve, step)
            powers(Block(NB + 2))
            results(Block(NB - 1))


_INS = ['x', 'src', 'edge_attr_128', 'L0_gnn_W1', 'L0_gnn_b1', 'L0_gnn_W2', 'L0_gnn_b2', 'L0_gnn_ln_gamma',
        'L0_gnn_ln_beta']


def kernel(**inputs):
    import numpy as _np
    import concourse.bacc as _bacc
    from concourse import mybir as _mybir
    from concourse.bass_utils import run_bass_kernel_spmd as _run

    nc = _bacc.Bacc("TRN2", target_bir_lowering=False, num_devices=1)
    arrays, args = {}, []
    for name in _INS:
        a = _np.ascontiguousarray(inputs[name])
        arrays[f"in_{name}_dram"] = a
        args.append(nc.dram_tensor(f"in_{name}_dram", a.shape, _mybir.dt.from_np(a.dtype), kind="ExternalInput").ap())
    shape = _np.asarray(inputs['x']).shape
    args.append(nc.dram_tensor("out_dram", shape, _mybir.dt.float32, kind="ExternalOutput").ap())
    gnn_layer(nc, *args)
    r = _run(nc, [arrays], core_ids=[0])
    return r.results[0]["out_dram"]
```

```python
from contextlib import ExitStack

import concourse.bass as bass
from concourse import mybir

F32 = mybir.dt.float32
F32R = mybir.dt.float32r
F16 = mybir.dt.float16
BF16 = mybir.dt.bfloat16
I32 = mybir.dt.int32
U32 = mybir.dt.uint32
ALU = mybir.AluOpType
ACT = mybir.ActivationFunctionType
AX = mybir.AxisListType

P = 128
TILES = 8
HALF = TILES // 2
BLOCK = P * TILES
RING = 3
X_RING = 6
X_AHEAD = 4
EPS = 1e-5
STREAMS = 4
PAIRS = 2
CAP = P // PAIRS
BIG = 128.0
BATCH = 7
UNROLL = 4 * BATCH
LAG_TABLE = 2 * BATCH
DVE_RANKS = (2, 9, 16)
LAG_DVE_RANK = 4
TURN_BLOCKS = 6
RSQRT_SEED = 0x5F3759DF
NEWTON = 3
OUTSIDE = 1 << 20


class Turn:

    def __init__(self, engine, i):
        self.engine, self.i, self.known = engine, i, {}

    def times(self, factor):
        if factor not in self.known:
            self.known[factor] = self.engine.snap(self.i * factor)
        return self.known[factor]


class Item:

    def __init__(self, n, stride=0, turn=None):
        self.n, self.stride, self.turn = n, stride, turn

    def plus(self, d):
        return Item(self.n + d, self.stride, self.turn)

    def ring(self, size):
        assert self.stride % size == 0
        return self.n % size

    def number(self, factor=1, more=0):
        fixed = factor * self.n + more
        return self.turn.times(factor * self.stride) + fixed if self.turn else fixed

    def group(self, size, factor=1, more=0):
        assert self.stride % size == 0
        fixed = factor * (self.n // size) + more
        return self.turn.times(factor * self.stride // size) + fixed if self.turn else fixed

    def exists(self, count):
        return self.turn is not None or 0 <= self.n < count

    def is_number(self, n):
        return self.turn is None and self.n == n


class Block(Item):

    @property
    def j(self):
        return self.ring(RING)

    @property
    def xj(self):
        return self.ring(X_RING)

    def x_lap(self, factor, more=0):
        return self.group(X_RING, factor, more)

    def plus(self, d):
        return Block(self.n + d, self.stride, self.turn)

    def lap(self, factor, more=0):
        return self.group(RING, factor, more)

    def half(self, c, factor=1, more=0):
        return self.number(2 * factor, factor * c + more)


def at_least(engine, semaphore, value, apart=None):
    if isinstance(value, int):
        if value > 0:
            engine.wait_ge(semaphore, value)
    else:
        engine.wait_ge(semaphore, value)
        if apart is not None:
            engine.sem_inc(apart)


def gnn_layer(nc, x, src, edge_attr, W1, b1, W2, b2, gamma, beta, out):
    nodes, D = x.shape
    edges = edge_attr.shape[0]
    H = W1.shape[1]
    assert D == P and H == 2 * P and nodes % TILES == 0
    NB = -(-nodes // BLOCK)
    LAST_ROWS = (nodes - (NB - 1) * BLOCK) // TILES
    NT = NB * TILES
    EC = -(-edges // P)
    FULL = edges // EC
    REST = edges - FULL * EC
    TURNS = EC // UNROLL
    FIRST_BLOCKS = 3
    assert all((place + LAG_DVE_RANK) % BATCH == BATCH - 1 for place in DVE_RANKS)
    assert EC % UNROLL == 0 and UNROLL % STREAMS == 0 and NT <= 512
    HEAD = 2
    LOOP_TURNS = (NB - 1 - HEAD - X_AHEAD) // TURN_BLOCKS
    TAIL = HEAD + LOOP_TURNS * TURN_BLOCKS
    GROUP = max(n for n in range(1, 129) if edges % n == 0)

    with ExitStack() as ctx:
        def sb(name, shape, dt):
            return ctx.enter_context(nc.sbuf_tensor(name, shape, dt))

        def psum(name, shape, dt=F32):
            return ctx.enter_context(nc.psum_tensor(name, shape, dt))

        def sem(name):
            return ctx.enter_context(nc.semaphore(name))

        spill = nc.dram_tensor("spill", (NB * BLOCK, D), F32, kind="Internal").ap()

        ident = sb("ident", [P, P], F32)
        ident16 = sb("ident16", [P, P], F16)
        swap16 = sb("swap16", [P, P], F16)
        before = sb("before", [P, P], F16)
        others = sb("others", [P, P], F16)
        zeros16 = sb("zeros16", [P, P], F16)
        ones16 = sb("ones16", [P, P], BF16)
        iota_tile = sb("iota_tile", [P, NT], F16)
        iota_slot = sb("iota_slot", [P, UNROLL, CAP], F16)
        iota_node = sb("iota_node", [P, P], F32)
        own_node = sb("own_node", [P, NT], F32)
        own_slot = sb("own_slot", [P, 1], F32)
        neg_big = sb("neg_big", [P, 1], F32)
        neg_cap = sb("neg_cap", [P, 1], F32)
        warm = sb("warm", [P, 1], F32)
        zeros_rank = sb("zeros_rank", [P, NT], BF16)

        srci = sb("srci", [P, EC], I32)
        tmp_a = sb("tmp_a", [P, EC], I32)
        tmp_b = sb("tmp_b", [P, EC], I32)
        tmp_c = sb("tmp_c", [P, EC], I32)
        edge_no = sb("edge_no", [P, EC], I32)
        tile_of = sb("tile_of", [P, EC], F32)
        word = sb("word", [P, EC, 2], F16)
        rank = sb("rank", [P, EC], F32)
        hot_tile = sb("hot_tile", [P, UNROLL, NT], F16)
        is_slot = sb("is_slot", [P, BATCH, CAP], F16)
        hot_slot = sb("hot_slot", [P, UNROLL, 2, CAP], F16)
        junk_rank = sb("junk_rank", [P, STREAMS, NT], BF16)
        junk_rank_dve = sb("junk_rank_dve", [P, NT], BF16)
        junk_excess = sb("junk_excess", [P, PAIRS, NT], BF16)
        counts_last = sb("counts_last", [P, PAIRS, NT], F16)
        total = sb("total", [P, PAIRS, NT], F16)
        excess = sb("excess", [P, PAIRS], F32)
        words = sb("words", [P, PAIRS, NT], F16)
        w2i = sb("w2i", [P, NT], I32)
        w2hi = sb("w2hi", [P, NT], I32)
        w2lo = sb("w2lo", [P, NT], I32)
        edge16 = sb("edge16", [P, NT], F32)
        edge_f = sb("edge_f", [P, NT], F32)
        empty = sb("empty", [P, NT], F32)
        own_part = sb("own_part", [P, NT], F32)
        slot_edge = sb("slot_edge", [P, NT], U32)
        slot_node = sb("slot_node", [P, NT], F32)
        spilled = sb("spilled", [P, 1], F32)
        kept = sb("kept", [P, 1], F32)
        spilled_i = sb("spilled_i", [P, 1], I32)

        w1f = sb("w1f", [P, 2, H], F32)
        w1h = sb("w1h", [P, 2, H], F32R)
        w1l = sb("w1l", [P, 2, H], F32R)
        w2f = sb("w2f", [P, 2, D], F32)
        w2c = sb("w2c", [P, 2, D], F32)
        w2sum = sb("w2sum", [P, 2], F32)
        b1c = sb("b1c", [P, 2], F32)
        b2f = sb("b2f", [P, D], F32)
        b2c = sb("b2c", [P, D], F32)
        b2sum = sb("b2sum", [P, 1], F32)
        b2p = [sb(f"b2p{i}", [P, D], BF16) for i in range(3)]
        b2r = [sb(f"b2r{i}", [P, D], F32) for i in range(2)]
        b2rows = sb("b2rows", [P, HALF, D], BF16)
        gammas = sb("gammas", [P, D], F32)
        betas = sb("betas", [P, D], F32)

        X = [sb(f"X{j}", [P, TILES, D], F32) for j in range(X_RING)]
        H0 = [sb(f"H0{j}", [P, TILES, D], F32) for j in range(RING)]
        R = [sb(f"R{j}", [P, TILES, D], F32) for j in range(RING)]
        G = [sb(f"G{j}", [P, TILES, D], F32) for j in range(RING)]
        HOT = [sb(f"HOT{j}", [P, TILES, P], F32) for j in range(RING)]
        gather_rows = [sb(f"gather_rows{j}", [P, TILES], U32) for j in range(RING)]
        hi = [sb(f"hi{c}", [P, 2, HALF * P], F32R) for c in range(2)]
        lo = [sb(f"lo{c}", [P, 2, HALF * P], F32R) for c in range(2)]
        S = [sb(f"S{c}", [P, 2, HALF * P], F32) for c in range(2)]
        T = [sb(f"T{c}", [P, HALF, D], F32) for c in range(2)]
        stats = [sb(f"stat{i}", [P, TILES, 6], F32) for i in range(2)]
        msum = sb("msum", [P, TILES], F32)
        mdif = sb("mdif", [P, TILES], F32)
        m2 = sb("m2", [P, TILES], F32)
        mdd = sb("mdd", [P, TILES], F32)
        var = sb("var", [P, 2 * TILES], F32)
        guess = [sb(f"guess{i}", [P, 2 * TILES], F32) for i in range(2)]
        guess_sq = sb("guess_sq", [P, 2 * TILES], F32)
        guess_off = sb("guess_off", [P, 2 * TILES], F32)
        rstd = [sb(f"rstd{j}", [P, 2 * TILES], F32) for j in range(RING)]
        shift = [sb(f"shift{j}", [P, TILES], F32) for j in range(RING)]
        meansq = [sb(f"meansq{j}", [P, TILES], F32) for j in range(RING)]
        junk_sq = sb("junk_sq", [P, 2, TILES, D], BF16)

        za = psum("za", [P, 2, HALF * P])
        pre = [psum(f"pre{m}", [P, 512]) for m in range(2)]
        y = [psum(f"y{i}", [P, 512]) for i in range(4)]
        table, slot_word = y[0:2], y[2:4]
        counts = [pre[0][:], pre[1][:], za[:, 0, :], za[:, 1, :]]

        src_loaded, weights_loaded = sem("src_loaded"), sem("weights_loaded")
        src_filled, slots_iota, late_const = sem("src_filled"), sem("slots_iota"), sem("late_const")
        pool_const, dve_const = sem("pool_const"), sem("dve_const")
        dve_step = sem("dve_step")
        w1h_ready, row_sums_ready, weights_ready = sem("w1h_ready"), sem("row_sums_ready"), sem("weights_ready")
        tile_hot, slot_step, slot_hot = sem("tile_hot"), sem("slot_step"), sem("slot_hot")
        counted, ranked, slot_free = sem("counted"), sem("ranked"), sem("slot_free")
        ranked_dve, totals_done, excess_known = sem("ranked_dve"), sem("totals_done"), sem("excess_known")
        counts_done, counts_copied = sem("counts_done"), sem("counts_copied")
        words_copied, words_placed = [sem(f"words_copied{i}") for i in range(PAIRS)], sem("words_placed")
        spill_known, slots_ready = sem("spill_known"), sem("slots_ready")
        pool_step = sem("pool_step")
        spill_zeroed, spill_added = sem("spill_zeroed"), sem("spill_added")
        rows_named = sem("rows_named")
        x_loaded = [sem(f"x_loaded{j}") for j in range(X_RING)]
        stored = [sem(f"stored{j}") for j in range(RING)]
        gathered = [[sem(f"gathered{j}{c}") for c in range(2)] for j in range(RING)]
        bn_done, small, powers_done = sem("bn_done"), sem("small"), sem("powers_done")
        h0_done, turn_done, hot_done, agg_done = sem("h0_done"), sem("turn_done"), sem("hot_done"), sem("agg_done")
        hi_done, lo_done = sem("hi_done"), sem("lo_done")
        pre_done, silu_done, y_done = sem("pre_done"), sem("silu_done"), sem("y_done")
        squares_done = sem("squares_done")
        xb_done, r_done, t_done, out_done = sem("xb_done"), sem("r_done"), sem("t_done"), sem("out_done")
        sp_passed, pool_passed = sem("sp_passed"), sem("pool_passed")

        def run_blocks(engine, step):
            for n in range(HEAD):
                step(Block(n))
            with engine.Fori(0, LOOP_TURNS) as i:
                turn = Turn(engine, i)
                for n in range(HEAD, HEAD + TURN_BLOCKS):
                    step(Block(n, TURN_BLOCKS, turn))
            for n in range(TAIL, NB):
                step(Block(n))

        def run_columns(engine, step, lag):
            for n in range(UNROLL):
                step(Item(n))
            with engine.Fori(0, TURNS - 1) as i:
                turn = Turn(engine, i)
                for n in range(UNROLL, 2 * UNROLL):
                    step(Item(n, UNROLL, turn))
            for n in range(EC, EC + lag):
                step(Item(n))

        def earlier(column, places, more=0):
            before_it = sum(place < column.ring(UNROLL) for place in places)
            return column.group(UNROLL, len(places), before_it + more)

        ACT_RANKS = [place for place in range(UNROLL) if place not in DVE_RANKS]
        block = ctx.enter_context(nc.Block())

        @block.sync
        def _(sp):
            sp.wait_ge(src_filled, 1)
            sp.dma_start(srci[0:FULL, :], src[0:FULL * EC].rearrange("(p c) -> p c", c=EC)).then_inc(src_loaded, 16)
            sp.dma_start(srci[FULL:FULL + 1, 0:REST],
                         src[FULL * EC:edges].rearrange("(p c) -> p c", p=1)).then_inc(src_loaded, 16)
            sp.dma_start(w1f[:], W1.rearrange("(k p) h -> p k h", p=P)).then_inc(weights_loaded, 16)
            sp.dma_start(w2f[:], W2.rearrange("(k p) d -> p k d", p=P)).then_inc(weights_loaded, 16)
            sp.dma_start(b1c[:], b1.rearrange("(k p) -> p k", p=P),
                         allow_slow_non_contiguous=True).then_inc(weights_loaded, 16)
            sp.dma_start(gammas[:], gamma.partition_broadcast(P)).then_inc(weights_loaded, 16)
            sp.dma_start(betas[:], beta.partition_broadcast(P)).then_inc(weights_loaded, 16)
            sp.dma_start(b2f[:], b2.partition_broadcast(P)).then_inc(weights_loaded, 16)

            def load(b):
                at_least(sp, h0_done, b.half(0, 1, 2 - 2 * X_RING), apart=sp_passed)
                at_least(sp, xb_done, b.half(0, 1, 2 - 2 * X_RING), apart=sp_passed)
                rows = LAST_ROWS if b.is_number(NB - 1) else P
                sp.dma_start(X[b.xj][0:rows], x[bass.ds(b.number(BLOCK), rows * TILES), :]
                             .rearrange("(p t) d -> p t d", t=TILES)).then_inc(x_loaded[b.xj], 16)

            def store(b):
                at_least(sp, out_done, b.half(0, 1, 2), apart=sp_passed)
                rows = LAST_ROWS if b.is_number(NB - 1) else P
                sp.dma_start(out[bass.ds(b.number(BLOCK), rows * TILES), :]
                             .rearrange("(p t) d -> p t d", t=TILES), R[b.j][0:rows]).then_inc(stored[b.j], 16)

            for n in range(X_AHEAD):
                load(Block(n))

            def step(b):
                if b.plus(X_AHEAD).exists(NB):
                    load(b.plus(X_AHEAD))
                if not b.is_number(0):
                    store(b.plus(-1))

            run_blocks(sp, step)
            last = Block(NB - 1)
            to = out[(NB - 1) * BLOCK:nodes, :].rearrange("(p t) d -> p t d", t=TILES)
            for c in range(2):
                s = slice(c * HALF, (c + 1) * HALF)
                sp.wait_ge(out_done, last.half(c, 1, 1))
                sp.dma_start(to[:, s, :], R[last.j][0:LAST_ROWS, s, :]).then_inc(stored[last.j], 16)
            for j in range(RING):
                sp.wait_ge(stored[j], 16 * (len(range(j, NB, RING)) + (j == last.j)))

        @block.gpsimd
        def _(pool):
            nc.gpsimd.memset(srci[:], OUTSIDE).then_inc(src_filled, 1)
            nc.gpsimd.memset(ident[:], 0.0).then_inc(pool_step, 1)
            nc.gpsimd.memset(before[:], 1.0).then_inc(pool_step, 1)
            pool.wait_ge(pool_step, 2)
            nc.gpsimd.affine_select(out=ident[:], in_=ident[:], compare_op=ALU.not_equal, fill=1.0, base=0,
                                    pattern=[[-1, P]], channel_multiplier=1).then_inc(pool_step, 1)
            nc.gpsimd.affine_select(out=before[:], in_=before[:], compare_op=ALU.is_gt, fill=0.0, base=0,
                                    pattern=[[1, P]], channel_multiplier=-1).then_inc(pool_step, 1)
            pool.wait_ge(pool_step, 4)
            nc.gpsimd.affine_select(out=before[:], in_=before[:], compare_op=ALU.not_equal, fill=BIG, base=0,
                                    pattern=[[-1, P]], channel_multiplier=1).then_inc(pool_step, 1)
            small_iota = dict(allow_small_or_imprecise_dtypes=True)
            nc.gpsimd.iota(edge_no[:], [[1, EC]], base=0, channel_multiplier=EC)
            done = nc.gpsimd.iota(iota_tile[:], [[1, NT]], base=0, channel_multiplier=0, **small_iota)
            done.then_inc(pool_const, 1)
            by_side = iota_slot[:].rearrange("p (a s b) r -> p a s b r", s=STREAMS // PAIRS, b=PAIRS)
            nc.gpsimd.iota(by_side[:, :, 0], [[0, UNROLL // STREAMS], [0, PAIRS], [1, CAP]],
                           base=0, channel_multiplier=0, **small_iota)
            nc.gpsimd.iota(by_side[:, :, 1], [[0, UNROLL // STREAMS], [0, PAIRS], [-1, CAP]],
                           base=CAP - 1, channel_multiplier=0, **small_iota).then_inc(slots_iota, 1)
            nc.gpsimd.tensor_copy(ident16[:], ident[:])
            nc.gpsimd.tensor_copy(swap16[:, 0:CAP], ident[:, CAP:P])
            nc.gpsimd.tensor_copy(swap16[:, CAP:P], ident[:, 0:CAP])
            nc.gpsimd.iota(iota_node[:], [[1, P]], base=0, channel_multiplier=0, **small_iota)
            nc.gpsimd.iota(own_slot[:], [[1, 1]], base=0, channel_multiplier=1, **small_iota)
            nc.gpsimd.iota(own_node[:], [[BLOCK, NB], [1, TILES]], base=0, channel_multiplier=TILES, **small_iota)
            for j in range(RING):
                done = nc.gpsimd.memset(G[j][:], 0.0)
            done.then_inc(late_const, 1)

            steps = [5]

            def link(instruction):
                steps[0] += 1
                instruction.then_inc(pool_step, 1)
                pool.wait_ge(pool_step, steps[0])

            pool.wait_ge(weights_loaded, 16 * 6)
            pool.wait_ge(row_sums_ready, 1)
            nc.gpsimd.tensor_scalar(out=b2r[0][:], in0=b2f[:], scalar1=float(D), scalar2=b2sum[:],
                                    op0=ALU.mult, op1=ALU.subtract)
            for m in range(2):
                nc.gpsimd.tensor_scalar(out=w2c[:, m, :], in0=w2f[:, m, :], scalar1=float(D),
                                        scalar2=w2sum[:, m:m + 1], op0=ALU.mult, op1=ALU.subtract)
            link(nc.gpsimd.memset(b2rows[:], 0.0))
            link(nc.gpsimd.tensor_scalar(out=w2c[:], in0=w2c[:], scalar1=1.0 / D, scalar2=None, op0=ALU.mult))
            link(nc.gpsimd.tensor_scalar(out=b2c[:], in0=b2r[0][:], scalar1=1.0 / D, scalar2=None, op0=ALU.mult))
            link(nc.gpsimd.tensor_copy(b2p[0][:], b2c[:]))
            link(nc.gpsimd.tensor_tensor(out=b2r[0][:], in0=b2c[:], in1=b2p[0][:], op=ALU.subtract))
            link(nc.gpsimd.tensor_copy(b2p[1][:], b2r[0][:]))
            link(nc.gpsimd.tensor_tensor(out=b2r[1][:], in0=b2r[0][:], in1=b2p[1][:], op=ALU.subtract))
            link(nc.gpsimd.tensor_copy(b2p[2][:], b2r[1][:]))
            for i in range(3):
                row = slice(32 * i, 32 * i + 1)
                for t in range(HALF):
                    done = nc.gpsimd.tensor_copy(b2rows[row, t, :], b2p[i][row, :])
            link(done)
            pool.wait_ge(w1h_ready, 1)
            nc.gpsimd.tensor_tensor(out=w1l[:], in0=w1f[:], in1=w1h[:].bitcast(F32),
                                    op=ALU.subtract).then_inc(weights_ready, 1)

            def x_plus_beta(b, c):
                pool.wait_ge(x_loaded[b.xj], b.x_lap(16, 16))
                at_least(pool, stored[b.j], b.lap(16))
                s = slice(c * HALF, (c + 1) * HALF)
                nc.gpsimd.tensor_tensor(out=R[b.j][:, s, :], in0=X[b.xj][:, s, :],
                                        in1=betas[:].unsqueeze(1).to_broadcast([P, HALF, D]),
                                        op=ALU.add).then_inc(xb_done, 1)

            for n in range(RING):
                for c in range(2):
                    x_plus_beta(Block(n), c)

            pool.wait_ge(spill_known, 1)
            flag = pool.value_load(spilled_i[0:1, 0:1], min_val=0, max_val=1)
            with pool.If(flag != 0):
                pool.wait_ge(late_const, 1)
                rows_zeroed = P * TILES
                with pool.Fori(0, NB) as n:
                    pool.dma_start(spill[bass.ds(n * rows_zeroed, rows_zeroed), :]
                                   .rearrange("(p t) d -> p t d", t=TILES), G[0][:]).then_inc(spill_zeroed, 16)
                pool.wait_ge(spill_zeroed, 16 * NB)
                with pool.Fori(0, edges // GROUP) as g:
                    first = pool.snap(g * GROUP)
                    with pool.Fori(0, GROUP) as i:
                        node = pool.value_load(src[bass.ds(first + i, 1)].rearrange("(a b) -> a b", a=1),
                                               min_val=0, max_val=nodes - 1)
                        pool.dma_start(spill[bass.ds(node, 1), :], edge_attr[bass.ds(first + i, 1), :],
                                       accum_op=ALU.add).then_inc(spill_added, 16)
                        at_least(pool, spill_added, i * 16 + 16, apart=pool_passed)
                    pool.dma_reset(range(spill_added.num, spill_added.num + 1))
                    pool.sem_clear(spill_added)

            def gather(b, c):
                at_least(pool, agg_done, b.half(0, 1, 2 - 2 * RING), apart=pool_passed)
                if b.is_number(FIRST_BLOCKS):
                    pool.wait_ge(slots_ready, 2)
                if c == 0:
                    nc.gpsimd.tensor_copy(gather_rows[b.j][:],
                                          slot_edge[:, bass.ds(b.number(TILES), TILES)]).then_inc(rows_named, 1)
                at_least(pool, rows_named, b.number(1, 1), apart=pool_passed)

                def rows_from(source, last):
                    for t in range(c * HALF, (c + 1) * HALF):
                        nc.gpsimd.indirect_dma_start(
                            G[b.j][:, t, :], None, source,
                            bass.IndirectOffsetOnAxis(ap=gather_rows[b.j][:, t:t + 1], axis=0),
                            bounds_check=last, oob_is_err=False).then_inc(gathered[b.j][c], 16)

                with pool.If(flag != 0):
                    rows_from(spill, NB * BLOCK - 1)
                with pool.If(flag == 0):
                    rows_from(edge_attr, edges - 1)

            pool.wait_ge(late_const, 1)
            pool.wait_ge(slots_ready, 1)
            for c in range(2):
                gather(Block(0), c)
            for c in range(2):
                gather(Block(1), c)

            def step(b):
                if b.plus(2).exists(NB):
                    gather(b.plus(2), 0)
                if b.plus(1).exists(NB) and not (b.turn is None and b.n + 1 < RING):
                    for c in range(2):
                        x_plus_beta(b.plus(1), c)
                if b.plus(2).exists(NB):
                    gather(b.plus(2), 1)

            run_blocks(pool, step)

        @block.scalar
        def _(act):
            act.wait_ge(dve_const, 1)
            nc.scalar.activation(warm[:], neg_big[:], ACT.Silu)

            def rank_of(column):
                if column.is_number(2 * BATCH - 1):
                    act.wait_ge(weights_loaded, 16 * 6)
                    nc.scalar.copy(w1h[:], w1f[:]).then_inc(w1h_ready, 1)
                if column.ring(UNROLL) in DVE_RANKS:
                    return
                s = column.ring(STREAMS)
                act.wait_ge(counted, column.number(1, 1))
                nc.scalar.activation(junk_rank[:, s, :], counts[s][:, 0:NT], ACT.Relu, bias=neg_big[:],
                                     accum_out=rank[:, bass.ds(column.number(), 1)]).then_inc(ranked, 1)

            run_columns(act, rank_of, 0)
            act.wait_ge(counts_done, 1)
            nc.scalar.copy(counts_last[:], za[:, :, 0:NT]).then_inc(counts_copied, 1)
            act.wait_ge(slot_free, EC + UNROLL)
            nc.scalar.copy(words[:, 1, :], table[1][:, 0:NT]).then_inc(words_copied[1], 1)
            for s in range(PAIRS):
                act.wait_ge(totals_done, s + 1)
                done = nc.scalar.activation(junk_excess[:, s, :], total[:, s, :], ACT.Relu, bias=neg_cap[:],
                                            accum_out=excess[:, s:s + 1])
            done.then_inc(excess_known, 1)

            def normalise(b, c):
                act.wait_ge(powers_done, b.number(1, 1))
                at_least(act, turn_done, b.half(c, 1, 1 - 2 * RING))
                at_least(act, r_done, b.half(c, 1, 1 - 2 * RING))
                for t in range(c * HALF, (c + 1) * HALF):
                    done = nc.scalar.activation(H0[b.j][:, t, :], X[b.xj][:, t, :], ACT.Relu,
                                                bias=shift[b.j][:, t:t + 1], scale=rstd[b.j][:, t:t + 1])
                done.then_inc(h0_done, 1)

            def split_high(b, c):
                act.wait_ge(turn_done, b.half(c, 1, 1))
                at_least(act, pre_done, b.half(c, 2, -2))
                nc.scalar.copy(hi[c][:, 0, :], za[:, 0, :])
                act.wait_ge(agg_done, b.half(c, 1, 1))
                nc.scalar.copy(hi[c][:, 1, :], za[:, 1, :]).then_inc(hi_done, 1)

            def silu(b, c):
                for m in range(2):
                    act.wait_ge(pre_done, b.half(c, 2, m + 1))
                    at_least(act, y_done, b.half(c, 1, -1))
                    nc.scalar.activation(S[c][:, m, :], pre[m][:], ACT.Silu, bias=b1c[:, m:m + 1]).then_inc(silu_done, 1)

            def squares(b, c):
                p = b.ring(2)
                act.wait_ge(y_done, b.half(c, 1, 1))
                for t in range(HALF):
                    done = nc.scalar.activation(junk_sq[:, p, c * HALF + t, :], y[2 * p + c][:, t * D:(t + 1) * D], ACT.Square,
                                                scale=float(D) ** -0.5,
                                                accum_out=meansq[b.j][:, c * HALF + t:c * HALF + t + 1])
                done.then_inc(squares_done, 1)

            for c in range(2):
                normalise(Block(0), c)
            split_high(Block(0), 0)

            def step(b):
                for c in range(2):
                    silu(b, c)
                    ahead = b.plus(1) if c else b
                    if ahead.exists(NB):
                        split_high(ahead, 1 - c)
                    if b.is_number(0) and c == 0:
                        normalise(b.plus(1), 0)
                    if b.plus(1 + c).exists(NB):
                        normalise(b.plus(1 + c), 1 - c)
                    squares(b, c)

            run_blocks(act, step)

        @block.tensor
        def _(pe):
            pe.wait_ge(dve_const, 2)
            for s in range(STREAMS):
                nc.tensor.matmul(counts[s][:, 0:NT], zeros16[:], iota_tile[:], start=True, stop=True)
            for s in range(PAIRS):
                done = nc.tensor.matmul(table[s][:, 0:NT], zeros16[:], iota_tile[:], start=True, stop=True)
            done.then_inc(slot_free, UNROLL)

            add = dict(start=False, stop=True, skip_group_check=True)

            def column_step(column):
                early, late = column.plus(-STREAMS), column.plus(-LAG_TABLE)
                if early.exists(EC):
                    if early.ring(UNROLL) in DVE_RANKS:
                        pe.wait_ge(ranked_dve, earlier(early, DVE_RANKS, 1))
                    else:
                        pe.wait_ge(ranked, earlier(early, ACT_RANKS, 1))
                    done = nc.tensor.matmul(counts[early.ring(STREAMS)][:, 0:NT], others[:],
                                            hot_tile[:, early.ring(UNROLL), :], **add)
                    if early.is_number(EC - 1):
                        done.then_inc(counts_done, 1)
                if column.exists(EC):
                    pe.wait_ge(tile_hot, column.number(1, 1))
                    nc.tensor.matmul(counts[column.ring(STREAMS)][:, 0:NT], before[:],
                                     hot_tile[:, column.ring(UNROLL), :], **add).then_inc(counted, 1)
                if late.exists(EC):
                    pe.wait_ge(slot_hot, late.group(BATCH, 1, 1))
                    nc.tensor.matmul(table[late.ring(PAIRS)][:, 0:NT],
                                     hot_slot[:, late.ring(UNROLL)].rearrange("p w r -> p (w r)"),
                                     hot_tile[:, late.ring(UNROLL), :], **add).then_inc(slot_free, 1)

            run_columns(pe, column_step, LAG_TABLE)

            for i in range(PAIRS):
                pe.wait_ge(words_copied[i], 1)
            pe.wait_ge(late_const, 1)
            for w in range(2):
                rows = slice(w * CAP, (w + 1) * CAP)
                for s in range(PAIRS):
                    to = ident16 if w == s else swap16
                    done = nc.tensor.matmul(slot_word[w][:, 0:NT], to[rows, :], words[rows, s, :],
                                            start=(s == 0), stop=(s == PAIRS - 1))
                done.then_inc(words_placed, 1)

            def turn_h(b, c):
                pe.wait_ge(h0_done, b.half(c, 1, 1))
                at_least(pe, hi_done, b.half(c))
                at_least(pe, lo_done, b.half(c))
                for t in range(HALF):
                    done = nc.tensor.transpose(za[:, 0, t * P:(t + 1) * P], H0[b.j][:, c * HALF + t, :], ident[:])
                done.then_inc(turn_done, 1)

            def sum_edges(b, c):
                pe.wait_ge(gathered[b.j][c], b.lap(16 * HALF, 16 * HALF))
                pe.wait_ge(hot_done, b.half(c, 1, 1))
                for t in range(HALF):
                    done = nc.tensor.matmul(za[:, 1, t * P:(t + 1) * P], G[b.j][:, c * HALF + t, :],
                                            HOT[b.j][:, c * HALF + t, :], start=True, stop=True)
                done.then_inc(agg_done, 1)

            def layer1(b, c):
                pe.wait_ge(hi_done, b.half(c, 1, 1))
                for m in range(2):
                    at_least(pe, silu_done, b.half(c, 2, m - 1))
                    cols = slice(m * P, (m + 1) * P)
                    for k in range(2):
                        nc.tensor.matmul(pre[m][:], w1h[:, k, cols], hi[c][:, k, :], start=(k == 0), stop=False)
                        nc.tensor.matmul(pre[m][:], w1l[:, k, cols], hi[c][:, k, :], start=False, stop=False)
                    if m == 0:
                        pe.wait_ge(lo_done, b.half(c, 1, 1))
                    for k in range(2):
                        done = nc.tensor.matmul(pre[m][:], w1h[:, k, cols], lo[c][:, k, :], start=False, stop=(k == 1))
                    done.then_inc(pre_done, 1)

            def layer2(b, c):
                place = y[2 * b.ring(2) + c]
                if b.is_number(1):
                    pe.wait_ge(slots_ready, 2)
                at_least(pe, t_done, b.half(c, 1, -3))
                nc.tensor.matmul(place[:], ones16[:], b2rows[:].rearrange("p t d -> p (t d)"), start=True, stop=False)
                pe.wait_ge(silu_done, b.half(c, 2, 2))
                for t in range(HALF):
                    for m in range(2):
                        done = nc.tensor.matmul(place[:, t * D:(t + 1) * D], S[c][:, m, t * P:(t + 1) * P],
                                                w2c[:, m, :], start=False, stop=(t == HALF - 1 and m == 1))
                done.then_inc(y_done, 1)

            pe.wait_ge(weights_ready, 1)
            pe.wait_ge(totals_done, 2)
            turn_h(Block(0), 0)
            sum_edges(Block(0), 0)

            def step(b):
                for c in range(2):
                    layer1(b, c)
                    ahead = b.plus(1) if c else b
                    if ahead.exists(NB):
                        turn_h(ahead, 1 - c)
                        sum_edges(ahead, 1 - c)
                    layer2(b, c)

            run_blocks(pe, step)

        @block.vector
        def _(dve):
            steps = [0]

            def link(instruction):
                steps[0] += 1
                instruction.then_inc(dve_step, 1)
                dve.wait_ge(dve_step, steps[0])

            nc.vector.memset(neg_cap[:], -float(CAP))
            nc.vector.memset(neg_big[:], -BIG).then_inc(dve_const, 1)
            nc.vector.memset(zeros_rank[:], 0.0)
            nc.vector.memset(zeros16[:], 0.0)
            nc.vector.memset(ones16[:], 1.0)
            for j in range(RING):
                nc.vector.memset(meansq[j][:], 1.0)
            dve.wait_ge(pool_const, 1)
            nc.vector.tensor_scalar(out=others[:], in0=before[:], scalar1=-1.0, scalar2=1.0,
                                    op0=ALU.mult, op1=ALU.add).then_inc(dve_const, 1)

            dve.wait_ge(src_loaded, 32)

            def bits(dst, a, s1, o1, s2, o2):
                return nc.vector.tensor_scalar(out=dst[:], in0=a[:], scalar1=s1, scalar2=s2, op0=o1, op1=o2)

            shr, shl, band = ALU.logical_shift_right, ALU.logical_shift_left, ALU.bitwise_and
            bits(tmp_a, srci, 10, shr, 3, shl)
            link(bits(tmp_b, srci, TILES - 1, band, None, ALU.bypass))
            link(nc.vector.tensor_tensor(out=tile_of[:], in0=tmp_a[:], in1=tmp_b[:], op=ALU.add))
            bits(tmp_a, srci, 3, shr, P - 1, band)
            link(bits(tmp_b, edge_no, 15, band, 7, shl))
            nc.vector.tensor_tensor(out=word[:, :, 1], in0=tmp_a[:], in1=tmp_b[:], op=ALU.add)
            link(bits(tmp_c, edge_no, 4, shr, None, ALU.bypass))
            link(nc.vector.tensor_scalar(out=word[:, :, 0], in0=tmp_c[:], scalar1=1.0, scalar2=None, op0=ALU.add))

            def statistics(b, t):
                if t == 0:
                    dve.wait_ge(x_loaded[b.xj], b.x_lap(16, 16))
                    at_least(dve, powers_done, b.number(1, -1))
                done = nc.vector.bn_stats(stats[b.ring(2)][:, t, :], X[b.xj][:, t, :])
                if t == TILES - 1:
                    done.then_inc(bn_done, 1)

            SMALLS = 4 + 3 * NEWTON

            def powers(b):
                count = [0]

                def link_small(instruction):
                    count[0] += 1
                    instruction.then_inc(small, 1)
                    place = count[0] - 1
                    if place == 0 and b.exists(NB) and not b.is_number(0):
                        one_hots(b, 0)
                    if 1 <= place <= TILES and b.plus(1).exists(NB):
                        statistics(b.plus(1), place - 1)
                    if place == TILES + 1 and b.plus(-1).exists(NB) and not b.is_number(1):
                        residual(b.plus(-1), 0)
                    dve.wait_ge(small, b.number(SMALLS, count[0]))

                stat = stats[b.ring(2)]
                at_least(dve, powers_done, b.number())
                if b.exists(NB):
                    dve.wait_ge(bn_done, b.number(1, 1))
                    nc.vector.tensor_tensor(out=msum[:], in0=stat[:, :, 1], in1=stat[:, :, 4], op=ALU.add)
                    nc.vector.scalar_tensor_tensor(out=m2[:], in0=stat[:, :, 2], scalar=EPS * D, in1=stat[:, :, 5],
                                                   op0=ALU.add, op1=ALU.add)
                link_small(nc.vector.tensor_tensor(out=mdif[:], in0=stat[:, :, 1], in1=stat[:, :, 4],
                                                   op=ALU.subtract))
                link_small(nc.vector.scalar_tensor_tensor(out=mdd[:], in0=mdif[:], scalar=0.25, in1=mdif[:],
                                                          op0=ALU.mult, op1=ALU.mult))
                at_least(dve, squares_done, b.half(0, 1, 2 - 2 * RING))
                nc.vector.tensor_scalar(out=var[:, TILES:], in0=meansq[b.j][:], scalar1=EPS, scalar2=None, op0=ALU.add)
                link_small(nc.vector.scalar_tensor_tensor(out=var[:, 0:TILES], in0=m2[:], scalar=1.0 / D, in1=mdd[:],
                                                          op0=ALU.mult, op1=ALU.add))
                link_small(nc.vector.tensor_scalar(out=guess[0][:].bitcast(I32), in0=var[:].bitcast(I32), scalar1=-0.5,
                                                   scalar2=float(RSQRT_SEED), op0=ALU.mult, op1=ALU.add))
                for i in range(NEWTON):
                    now = guess[i % 2]
                    then = rstd[b.j] if i == NEWTON - 1 else guess[(i + 1) % 2]
                    link_small(nc.vector.scalar_tensor_tensor(out=guess_sq[:], in0=now[:], scalar=-0.5, in1=now[:],
                                                              op0=ALU.mult, op1=ALU.mult))
                    link_small(nc.vector.tensor_tensor(out=guess_off[:], in0=guess_sq[:], in1=var[:], op=ALU.mult))
                    link_small(nc.vector.scalar_tensor_tensor(out=then[:], in0=guess_off[:], scalar=1.5, in1=now[:],
                                                              op0=ALU.add, op1=ALU.mult))
                nc.vector.scalar_tensor_tensor(out=shift[b.j][:], in0=msum[:], scalar=-0.5, in1=rstd[b.j][:, 0:TILES],
                                               op0=ALU.mult, op1=ALU.mult).then_inc(powers_done, 1)

            def rank_of(column):
                at_least(dve, ranked_dve, earlier(column, DVE_RANKS))
                dve.wait_ge(counted, column.number(1, 1))
                nc.vector.scalar_tensor_tensor(
                    out=junk_rank_dve[:], in0=counts[column.ring(STREAMS)][:, 0:NT], scalar=-BIG, in1=zeros_rank[:],
                    op0=ALU.add, op1=ALU.max,
                    accum_out=rank[:, bass.ds(column.number(), 1)]).then_inc(ranked_dve, 1)

            def column_step(column):
                if column.exists(EC):
                    dve.wait_ge(slot_free, column.number(1, 1))
                    nc.vector.tensor_scalar(out=hot_tile[:, column.ring(UNROLL), :], in0=iota_tile[:],
                                            scalar1=tile_of[:, bass.ds(column.number(), 1)], scalar2=None,
                                            op0=ALU.is_equal).then_inc(tile_hot, 1)
                late = column.plus(1 - 2 * BATCH)
                place = late.ring(UNROLL)
                batch = column.ring(BATCH) == BATCH - 1 and late.exists(EC)
                if batch:
                    if late.is_number(0):
                        dve.wait_ge(slots_iota, 1)
                    dve.wait_ge(ranked, earlier(late.plus(BATCH), ACT_RANKS))
                    at_least(dve, ranked_dve, earlier(late.plus(BATCH), DVE_RANKS))
                    at_least(dve, slot_hot, late.group(BATCH))
                    nc.vector.tensor_tensor(
                        out=is_slot[:], in0=iota_slot[:, place:place + BATCH],
                        in1=rank[:, bass.ds(late.number(), BATCH)].unsqueeze(2).to_broadcast([P, BATCH, CAP]),
                        op=ALU.is_equal).then_inc(slot_step, 1)
                ranking = column.plus(-LAG_DVE_RANK)
                if ranking.exists(EC) and ranking.ring(UNROLL) in DVE_RANKS:
                    rank_of(ranking)
                if batch:
                    dve.wait_ge(slot_step, late.group(BATCH, 1, 1))
                    nc.vector.tensor_tensor(
                        out=hot_slot[:, place:place + BATCH],
                        in0=is_slot[:].unsqueeze(2).to_broadcast([P, BATCH, 2, CAP]),
                        in1=word[:, bass.ds(late.number(), BATCH), :].unsqueeze(3).to_broadcast([P, BATCH, 2, CAP]),
                        op=ALU.mult).then_inc(slot_hot, 1)
                if column.is_number(2 * BATCH - 1):
                    dve.wait_ge(weights_loaded, 16 * 6)
                    nc.vector.tensor_reduce(out=b2sum[:], in_=b2f[:], axis=AX.X, op=ALU.add)
                    nc.vector.tensor_reduce(out=w2sum[:], in_=w2f[:], axis=AX.X,
                                            op=ALU.add).then_inc(row_sums_ready, 1)
                if column.is_number(EC):
                    for t in range(TILES):
                        statistics(Block(0), t)

            run_columns(dve, column_step, BATCH)

            dve.wait_ge(counts_copied, 1)
            for s in range(PAIRS):
                nc.vector.tensor_tensor(out=total[:, s, :], in0=counts[s][:, 0:NT], in1=counts_last[:, s, :],
                                        op=ALU.add).then_inc(totals_done, 1)
            dve.wait_ge(slot_free, EC + UNROLL)
            nc.vector.tensor_copy(words[:, 0, :], table[0][:, 0:NT]).then_inc(words_copied[0], 1)

            dve.wait_ge(excess_known, 1)
            dve.wait_ge(late_const, 1)
            link(nc.vector.tensor_scalar(out=spilled[:], in0=excess[:, 0:1], scalar1=excess[:, 1:2], scalar2=0.5,
                                         op0=ALU.add, op1=ALU.is_ge))
            nc.vector.tensor_copy(spilled_i[:], spilled[:]).then_inc(spill_known, 1)
            nc.vector.tensor_scalar(out=kept[:], in0=spilled[:], scalar1=-1.0, scalar2=1.0,
                                    op0=ALU.mult, op1=ALU.add)
            nc.vector.tensor_tensor(out=own_slot[:], in0=own_slot[:], in1=spilled[:], op=ALU.mult)

            def slot_tables(lo, hi):
                at = slice(lo, hi)
                nc.vector.tensor_copy(w2i[:, at], slot_word[1][:, at])
                nc.vector.tensor_scalar(out=own_part[:, at], in0=own_node[:, at], scalar1=spilled[:], scalar2=None,
                                        op0=ALU.mult)
                nc.vector.tensor_scalar(out=empty[:, at], in0=slot_word[0][:, at], scalar1=0.0,
                                        scalar2=float(1 << 17), op0=ALU.is_equal, op1=ALU.mult)
                link(nc.vector.tensor_scalar(out=edge16[:, at], in0=slot_word[0][:, at], scalar1=-1.0, scalar2=16.0,
                                             op0=ALU.add, op1=ALU.mult))
                nc.vector.tensor_scalar(out=w2hi[:, at], in0=w2i[:, at], scalar1=7, scalar2=None, op0=shr,
                                        op1=ALU.bypass)
                link(nc.vector.tensor_scalar(out=w2lo[:, at], in0=w2i[:, at], scalar1=P - 1, scalar2=None, op0=band,
                                             op1=ALU.bypass))
                nc.vector.tensor_tensor(out=edge_f[:, at], in0=edge16[:, at], in1=w2hi[:, at], op=ALU.add)
                link(nc.vector.tensor_tensor(out=slot_node[:, at], in0=empty[:, at], in1=w2lo[:, at], op=ALU.add))
                link(nc.vector.tensor_tensor(out=edge_f[:, at], in0=edge_f[:, at], in1=empty[:, at], op=ALU.add))
                nc.vector.tensor_scalar(out=slot_node[:, at], in0=slot_node[:, at], scalar1=kept[:],
                                        scalar2=own_slot[:], op0=ALU.mult, op1=ALU.add)
                nc.vector.scalar_tensor_tensor(out=slot_edge[:, at], in0=edge_f[:, at], scalar=kept[:],
                                               in1=own_part[:, at], op0=ALU.mult, op1=ALU.add).then_inc(slots_ready, 1)

            dve.wait_ge(words_placed, 2)
            slot_tables(0, FIRST_BLOCKS * TILES)


            def one_hots(b, c):
                if b.is_number(FIRST_BLOCKS) and c == 0:
                    dve.wait_ge(slots_ready, 2)
                at_least(dve, agg_done, b.half(0, 1, 2 - 2 * RING))
                nc.vector.tensor_tensor(
                    out=HOT[b.j][:, c * HALF:(c + 1) * HALF, :],
                    in0=iota_node[:].unsqueeze(1).to_broadcast([P, HALF, P]),
                    in1=slot_node[:, bass.ds(b.number(TILES, c * HALF), HALF)].unsqueeze(2).to_broadcast([P, HALF, P]),
                    op=ALU.is_equal).then_inc(hot_done, 1)

            def split_low(b, c):
                dve.wait_ge(hi_done, b.half(c, 1, 1))
                at_least(dve, pre_done, b.half(c, 2, -2))
                nc.vector.tensor_tensor(out=lo[c][:], in0=za[:], in1=hi[c][:].bitcast(F32),
                                        op=ALU.subtract).then_inc(lo_done, 1)

            def residual(b, c):
                dve.wait_ge(xb_done, b.half(c, 1, 1))
                dve.wait_ge(h0_done, b.half(c, 1, 1))
                s = slice(c * HALF, (c + 1) * HALF)
                nc.vector.tensor_tensor(out=R[b.j][:, s, :], in0=H0[b.j][:, s, :], in1=R[b.j][:, s, :],
                                        op=ALU.add).then_inc(r_done, 1)

            def scale(b, c):
                dve.wait_ge(powers_done, b.number(1, 1 + RING))
                at_least(dve, out_done, b.half(c, 1, -1))
                for t in range(HALF):
                    n = TILES + c * HALF + t
                    done = nc.vector.scalar_tensor_tensor(
                        out=T[c][:, t, :], in0=y[2 * b.ring(2) + c][:, t * D:(t + 1) * D],
                        scalar=rstd[b.j][:, n:n + 1], in1=gammas[:], op0=ALU.mult, op1=ALU.mult)
                done.then_inc(t_done, 1)

            def result(b, c):
                dve.wait_ge(t_done, b.half(c, 1, 1))
                dve.wait_ge(r_done, b.half(c, 1, 1))
                s = slice(c * HALF, (c + 1) * HALF)
                nc.vector.tensor_tensor(out=R[b.j][:, s, :], in0=T[c][:], in1=R[b.j][:, s, :],
                                        op=ALU.add).then_inc(out_done, 1)

            dve.wait_ge(slots_ready, 1)
            one_hots(Block(0), 0)
            powers(Block(0))
            one_hots(Block(0), 1)
            split_low(Block(0), 0)
            powers(Block(1))
            one_hots(Block(1), 1)
            for c in range(2):
                residual(Block(0), c)

            def step(b):
                split_low(b, 1)
                powers(b.plus(2))
                if b.plus(1).exists(NB):
                    split_low(b.plus(1), 0)
                if b.is_number(0):
                    slot_tables(FIRST_BLOCKS * TILES, NT)
                else:
                    for c in range(2):
                        scale(b.plus(-1), c)
                    for c in range(2):
                        result(b.plus(-1), c)
                if b.plus(2).exists(NB):
                    one_hots(b.plus(2), 1)
                if b.plus(1).exists(NB):
                    residual(b.plus(1), 1)

            run_blocks(dve, step)
            powers(Block(NB + 2))
            for c in range(2):
                scale(Block(NB - 1), c)
                result(Block(NB - 1), c)


_INS = ['x', 'src', 'edge_attr_128', 'L0_gnn_W1', 'L0_gnn_b1', 'L0_gnn_W2', 'L0_gnn_b2', 'L0_gnn_ln_gamma',
        'L0_gnn_ln_beta']


def kernel(**inputs):
    import numpy as _np
    import concourse.bacc as _bacc
    from concourse import mybir as _mybir
    from concourse.bass_utils import run_bass_kernel_spmd as _run

    nc = _bacc.Bacc("TRN2", target_bir_lowering=False, num_devices=1)
    arrays, args = {}, []
    for name in _INS:
        a = _np.ascontiguousarray(inputs[name])
        arrays[f"in_{name}_dram"] = a
        args.append(nc.dram_tensor(f"in_{name}_dram", a.shape, _mybir.dt.from_np(a.dtype), kind="ExternalInput").ap())
    shape = _np.asarray(inputs['x']).shape
    args.append(nc.dram_tensor("out_dram", shape, _mybir.dt.float32, kind="ExternalOutput").ap())
    gnn_layer(nc, *args)
    r = _run(nc, [arrays], core_ids=[0])
    return r.results[0]["out_dram"]
```
